# Optimizing a Trainium2 kernel written in Bass

```python
import numpy as np
import jax
import jax.numpy as jnp

def _softmax(x, axis=-1):
    return jax.nn.softmax(x, axis=axis)

def _gelu(x):
    return jax.nn.gelu(x, approximate=True)

def _silu(x):
    return jax.nn.silu(x)

def _sigmoid(x):
    return jax.nn.sigmoid(x)

def _layernorm(x, axis=-1, eps=1e-05):
    m = jnp.mean(x, axis=axis, keepdims=True)
    v = jnp.var(x, axis=axis, keepdims=True)
    return (x - m) / jnp.sqrt(v + eps)

def _scatter_add(tgt, idx, src, axis=0):
    return tgt.at[idx].add(src)

def _segment_sum(src, seg, n):
    return jax.ops.segment_sum(src, seg, n)
kernel_name = 'mk_lm_tower_d1_tok_ids512_r4_2d9d74'

def setup_inputs(seed: int=0):
    np.random.seed(seed)
    _w = jnp.asarray

    def _rec_inputs():
        import jax
        import jax.numpy as jnp
        _rk = jax.random.key(seed)
        x = jax.random.randint(jax.random.fold_in(_rk, 1), (16, 256), 0, 8000, jnp.int32)
        return x
    x = _rec_inputs()

    def _L0_tok_setup():
        import jax, jax.numpy as jnp
        import numpy as np
        VOCAB = 8000
        EMB = 128
        K = 3
        B, T = (8, 1024)
        key = jax.random.key(seed)
        k_ids, k_w = jax.random.split(key)
        token_ids = jax.random.randint(k_ids, (B, T), 0, VOCAB, dtype=jnp.int64)
        conv_w = jax.random.normal(k_w, (EMB, VOCAB, K), dtype=jnp.float32) * 0.02
        return {'token_ids': token_ids, 'conv_w': conv_w}
    _L0_tok_all = _L0_tok_setup()
    _L0_tok_in = {k: v for k, v in _L0_tok_all.items() if k in ('conv_w',)}
    del _L0_tok_all

    def _L0_attn_setup():
        import jax, jax.numpy as jnp
        import numpy as np
        import math
        D_MODEL = 128
        SLOPE = 0.5
        key = jax.random.key(seed)
        k1, k2, k3, k4 = jax.random.split(key, 4)
        B, S, D = (4, 1024, D_MODEL)
        x = jax.random.normal(k1, (B, S, D), dtype=jnp.float32)
        lim = 1.0 / math.sqrt(D)
        W_qk = jax.random.uniform(k2, (D, D), jnp.float32, -lim, lim)
        W_v = jax.random.uniform(k3, (D, D), jnp.float32, -lim, lim)
        b_v = jax.random.uniform(k4, (D,), jnp.float32, -lim, lim)
        return {'x': x, 'W_qk': W_qk, 'W_v': W_v, 'b_v': b_v}
    _L0_attn_all = _L0_attn_setup()
    _L0_attn_in = {k: v for k, v in _L0_attn_all.items() if k in ('W_qk', 'W_v', 'b_v')}
    del _L0_attn_all

    def _L0_ffn_setup():
        import jax, jax.numpy as jnp
        import numpy as np
        G = 4
        EPG = 4
        E = 16
        KG = 2
        K = 2
        GTP = 0.9
        TP = 0.9
        SCALE = 1.0 / float(np.sqrt(G))

        def _routing_weights(xf, Wr, br, Wgate, bgate):
            N = xf.shape[0]
            gp = jax.nn.softmax(xf @ Wr + br, axis=-1)
            order = jnp.argsort(-gp, axis=-1)
            sp_k = jnp.take_along_axis(gp, order, axis=-1)[:, :KG]
            idx_k = order[:, :KG]
            act = jnp.cumsum(sp_k, axis=-1) <= GTP
            act = act.at[:, 0].set(True)
            mp = sp_k * act
            rn = mp / (jnp.sum(mp, axis=-1, keepdims=True) + 1e-09)
            w_group = jnp.zeros((N, G), xf.dtype).at[jnp.arange(N)[:, None], idx_k].set(rn)
            ep = jax.nn.softmax(jnp.einsum('nd,gde->nge', xf, Wgate) + bgate, axis=-1)
            eorder = jnp.argsort(-ep, axis=-1)
            esp = jnp.take_along_axis(ep, eorder, axis=-1)[:, :, :K]
            eidx = eorder[:, :, :K]
            eact = jnp.cumsum(esp, axis=-1) <= TP
            eact = eact.at[:, :, 0].set(True)
            emp = esp * eact
            ern = emp / (jnp.sum(emp, axis=-1, keepdims=True) + 1e-09)
            w_exp = jnp.zeros((N, G, EPG), xf.dtype).at[jnp.arange(N)[:, None, None], jnp.arange(G)[None, :, None], eidx].set(ern)
            return (w_group[:, :, None] * w_exp * SCALE).reshape(N, E)
        key = jax.random.key(seed)
        ks = jax.random.split(key, 6)
        B, T, D, H = (2, 256, 128, 512)
        x = jax.random.normal(ks[0], (B, T, D), jnp.float32)
        Wr = jax.random.normal(ks[1], (D, G), jnp.float32) * 0.02
        br = jnp.zeros((G,), jnp.float32)
        Wgate = jax.random.normal(ks[2], (G, D, EPG), jnp.float32) * 0.02
        bgate = jnp.zeros((G, EPG), jnp.float32)
        W1 = jax.random.normal(ks[3], (E, D, H), jnp.float32) * 0.02
        W3 = jax.random.normal(ks[4], (E, D, H), jnp.float32) * 0.02
        W2 = jax.random.normal(ks[5], (E, H, D), jnp.float32) * 0.02
        return {'x': x, 'Wr': Wr, 'br': br, 'Wgate': Wgate, 'bgate': bgate, 'W1': W1, 'W3': W3, 'W2': W2}
    _L0_ffn_all = _L0_ffn_setup()
    _L0_ffn_in = {k: v for k, v in _L0_ffn_all.items() if k in ('Wr', 'br', 'Wgate', 'bgate', 'W1', 'W3', 'W2')}
    del _L0_ffn_all
    return {'x': x, 'L0_tok_conv_w': _L0_tok_in['conv_w'], 'L0_attn_W_qk': _L0_attn_in['W_qk'], 'L0_attn_W_v': _L0_attn_in['W_v'], 'L0_attn_b_v': _L0_attn_in['b_v'], 'L0_ffn_Wr': _L0_ffn_in['Wr'], 'L0_ffn_br': _L0_ffn_in['br'], 'L0_ffn_Wgate': _L0_ffn_in['Wgate'], 'L0_ffn_bgate': _L0_ffn_in['bgate'], 'L0_ffn_W1': _L0_ffn_in['W1'], 'L0_ffn_W3': _L0_ffn_in['W3'], 'L0_ffn_W2': _L0_ffn_in['W2']}

def reference(x, L0_tok_conv_w, L0_attn_W_qk, L0_attn_W_v, L0_attn_b_v, L0_ffn_Wr, L0_ffn_br, L0_ffn_Wgate, L0_ffn_bgate, L0_ffn_W1, L0_ffn_W3, L0_ffn_W2):
    import jax
    import jax.numpy as jnp

    def _L0_tok_ref(token_ids, conv_w):
        import jax, jax.numpy as jnp
        import numpy as np
        VOCAB = 8000
        EMB = 128
        K = 3
        B, T = (8, 1024)
        'Equivalent to one_hot(token_ids) -> Conv1d(V->F, k=K, pad=K//2, no bias).\n\n            Because the conv input is one-hot over the vocab channel, the V-dim\n            contraction reduces to gathering one weight row per (position, tap):\n              out[b,t,f] = sum_k W[f, token[b, t+k-pad], k]   (zero outside [0,T)).\n            '
        Bn, Tn = token_ids.shape
        F_, V_, Kn = conv_w.shape
        pad = Kn // 2
        out = jnp.zeros((Bn, Tn, F_), dtype=conv_w.dtype)
        t = jnp.arange(Tn)
        for k in range(Kn):
            shift = k - pad
            src = t + shift
            valid = (src >= 0) & (src < Tn)
            src_c = jnp.clip(src, 0, Tn - 1)
            ids = token_ids[:, src_c]
            table_k = conv_w[:, :, k].T
            emb = table_k[ids]
            out = out + jnp.where(valid[None, :, None], emb, jnp.zeros((), conv_w.dtype))
        return out

    def _L0_attn_ref(x, W_qk, W_v, b_v):
        import jax, jax.numpy as jnp
        import numpy as np
        import math
        D_MODEL = 128
        SLOPE = 0.5
        B, S, D = x.shape
        scale = 1.0 / math.sqrt(D)
        scores = jnp.einsum('bid,de,bje->bij', x, W_qk, x) * scale
        i = jnp.arange(S, dtype=x.dtype)[:, None]
        j = jnp.arange(S, dtype=x.dtype)[None, :]
        scores = scores + (j - i) * jnp.asarray(SLOPE, x.dtype)
        causal = j > i
        scores = jnp.where(causal, -jnp.inf, scores)
        attn = jax.nn.softmax(scores, axis=-1)
        v = jnp.einsum('bjd,ed->bje', x, W_v) + b_v
        return jnp.einsum('bij,bje->bie', attn, v)

    def _L0_ffn_ref(x, Wr, br, Wgate, bgate, W1, W3, W2):
        import jax, jax.numpy as jnp
        import numpy as np
        G = 4
        EPG = 4
        E = 16
        KG = 2
        K = 2
        GTP = 0.9
        TP = 0.9
        SCALE = 1.0 / float(np.sqrt(G))

        def _routing_weights(xf, Wr, br, Wgate, bgate):
            N = xf.shape[0]
            gp = jax.nn.softmax(xf @ Wr + br, axis=-1)
            order = jnp.argsort(-gp, axis=-1)
            sp_k = jnp.take_along_axis(gp, order, axis=-1)[:, :KG]
            idx_k = order[:, :KG]
            act = jnp.cumsum(sp_k, axis=-1) <= GTP
            act = act.at[:, 0].set(True)
            mp = sp_k * act
            rn = mp / (jnp.sum(mp, axis=-1, keepdims=True) + 1e-09)
            w_group = jnp.zeros((N, G), xf.dtype).at[jnp.arange(N)[:, None], idx_k].set(rn)
            ep = jax.nn.softmax(jnp.einsum('nd,gde->nge', xf, Wgate) + bgate, axis=-1)
            eorder = jnp.argsort(-ep, axis=-1)
            esp = jnp.take_along_axis(ep, eorder, axis=-1)[:, :, :K]
            eidx = eorder[:, :, :K]
            eact = jnp.cumsum(esp, axis=-1) <= TP
            eact = eact.at[:, :, 0].set(True)
            emp = esp * eact
            ern = emp / (jnp.sum(emp, axis=-1, keepdims=True) + 1e-09)
            w_exp = jnp.zeros((N, G, EPG), xf.dtype).at[jnp.arange(N)[:, None, None], jnp.arange(G)[None, :, None], eidx].set(ern)
            return (w_group[:, :, None] * w_exp * SCALE).reshape(N, E)
        B, T, D = x.shape
        xf = x.reshape(-1, D)
        tw = _routing_weights(xf, Wr, br, Wgate, bgate)
        out = jnp.zeros_like(xf)
        for e in range(E):
            h = jax.nn.silu(xf @ W1[e]) * (xf @ W3[e])
            out = out + tw[:, e:e + 1] * (h @ W2[e])
        return out.reshape(B, T, D)
    h = _L0_tok_ref(x, L0_tok_conv_w)
    h = h + _L0_attn_ref(_layernorm(h, axis=-1), L0_attn_W_qk, L0_attn_W_v, L0_attn_b_v)
    h = h + _L0_ffn_ref(_layernorm(h, axis=-1), L0_ffn_Wr, L0_ffn_br, L0_ffn_Wgate, L0_ffn_bgate, L0_ffn_W1, L0_ffn_W3, L0_ffn_W2)
    return h

_drawn_inputs = setup_inputs


def setup_inputs(seed=0):
    import zlib

    import numpy as np

    out = dict(_drawn_inputs(seed))
    spreads = {'L0_ffn_br': (0.0, 0.8), 'L0_ffn_bgate': (0.0, 0.8)}
    factors = {'L0_ffn_Wr': 8.0,
     'L0_ffn_Wgate': 8.0,
     'L0_ffn_W1': 6.054,
     'L0_ffn_W3': 6.013,
     'L0_ffn_W2': 6.022}
    for name, (base, spread) in spreads.items():
        noise = np.random.default_rng([zlib.crc32(name.encode()), seed]).standard_normal(out[name].shape)
        drawn = base * np.exp(spread * noise) if base else spread * noise
        out[name] = jnp.asarray(drawn.astype(out[name].dtype))
    for name, factor in factors.items():
        out[name] = (out[name] * factor).astype(out[name].dtype)
    return out
```

```python
from contextlib import ExitStack

import concourse.bass as bass
from concourse import mybir

F32 = mybir.dt.float32
BF16 = mybir.dt.bfloat16
I32 = mybir.dt.int32
ALU = mybir.AluOpType
ACT = mybir.ActivationFunctionType
AX = mybir.AxisListType

P = 128
D = 128
TAPS = 3
VOCAB = 8000
BATCHES, SEQ = 16, 256
TOKENS = BATCHES * SEQ
TILES_IN = TOKENS // P
CHUNKS = 4
TC = TILES_IN // CHUNKS
BC = BATCHES // CHUNKS
GROUPS, PER_GROUP = 4, 4
EXPERTS = GROUPS * PER_GROUP
SETS = GROUPS + 1
SLOTS = 4
HID = 512
HK = HID // P
KEEP = 0.9
EPS = 1e-5
SCALE = float(D) ** -0.5
SLOPE = 0.5
MASKED = -3.0e38

REC = D + 2
REGION = TOKENS + P
TILES = 144
SPARE = TILES - TOKENS * SLOTS // P
SENT_ROWS = EXPERTS * REGION + SPARE * P
RING = 4
AHEAD = TILES - RING

VECTOR_BEFORE = 0
VECTOR_PER_CHUNK = 44


def tower_kernel(nc, ids, embedding, w_qk, w_v_t, b_v, w_route, w_gate, b_route, b_gate, w1, w3, w2, out):
    ctx = ExitStack()
    with ctx:
        def sb(name, shape, dt=F32):
            return ctx.enter_context(nc.sbuf_tensor(name, shape, dt))

        def sem(name):
            return ctx.enter_context(nc.semaphore(name))

        bank = [ctx.enter_context(nc.psum_tensor(f"bank{n}", [P, 512], F32)) for n in range(8)]

        sent = nc.dram_tensor("sent", [SENT_ROWS, REC], F32, kind="Internal").ap()
        sums = [nc.dram_tensor(f"sums{n}", [TOKENS + P, D], F32, kind="Internal").ap() for n in range(2)]

        ident = sb("ident", [P, P])
        from_before = sb("from_before", [P, P])
        from_after = sb("from_after", [P, P])
        last_to_first = sb("last_to_first", [P, P])
        first_to_last = sb("first_to_last", [P, P])
        earlier = sb("earlier", [P, P], BF16)
        ones = sb("ones", [P, P], BF16)
        position_bias = sb("position_bias", [P, 3 * P])
        eps = sb("eps", [P, 1])
        zeros = sb("zeros", [P, D])
        pad_rows = sb("pad_rows", [P, REC])
        token_number = sb("token_number", [P, TILES_IN])
        region_start = sb("region_start", [P, EXPERTS])
        tile_number = sb("tile_number", [1, TILES])
        ones_row = sb("ones_row", [1, EXPERTS])

        ids_sb = sb("ids_sb", [P, TILES_IN], I32)
        wqk_sb = sb("wqk_sb", [P, D])
        wvt_sb = sb("wvt_sb", [P, D])
        bv_sb = sb("bv_sb", [P, D])
        router_w = sb("router_w", [P, SETS * PER_GROUP])
        router_b = sb("router_b", [P, SETS * PER_GROUP])
        w1_sb = sb("w1_sb", [P, EXPERTS * HID])
        w3_sb = sb("w3_sb", [P, EXPERTS * HID])
        w2_sb = sb("w2_sb", [P, EXPERTS * HID])

        gather_ids = sb("gather_ids", [P, TC], I32)
        taps = sb("taps", [P, TC, TAPS * D])
        h = sb("h", [P, TC, D])
        stats = sb("stats", [P, TC, 6])
        mean = sb("mean", [P, TC])
        var = sb("var", [P, TC])
        std = sb("std", [P, TC])
        rstd = sb("rstd", [P, TC])
        xn = sb("xn", [P, TC, D])
        xT = sb("xT", [P, 2, SEQ])
        qT = sb("qT", [P, 2, SEQ])
        v = sb("v", [P, 2, SEQ])
        scores = sb("scores", [P, 2, 3 * P])
        neg_max = sb("neg_max", [P, 2, 2])
        probs = sb("probs", [P, 2, 3 * P])
        row_sum = sb("row_sum", [P, 2, 2])
        row_inv = sb("row_inv", [P, 2, 2])
        pT = sb("pT", [P, 2, 3 * P])
        h1 = sb("h1", [P, TC, D])
        stats2 = sb("stats2", [P, TC, 6])
        half_sums = sb("half_sums", [P, 4, TC])
        std2 = sb("std2", [P, TC])
        rstd2 = sb("rstd2", [P, TC])
        rows = sb("rows", [P, TC, SLOTS, REC])
        x2T = sb("x2T", [P, TC * P])

        NS = TC * SETS
        logits = sb("logits", [P, NS, PER_GROUP])
        set_max = sb("set_max", [P, NS])
        shifted = sb("shifted", [P, NS, PER_GROUP])
        choice = sb("choice", [P, NS, PER_GROUP])
        set_sum = sb("set_sum", [P, NS])
        set_inv = sb("set_inv", [P, NS])
        beats = sb("beats", [P, NS, 6])
        part = sb("part", [P, NS, PER_GROUP])
        rank = sb("rank", [P, NS, PER_GROUP])
        is_first = sb("is_first", [P, NS, PER_GROUP])
        is_second = sb("is_second", [P, NS, PER_GROUP])
        p_first = sb("p_first", [P, NS])
        p_second = sb("p_second", [P, NS])
        both = sb("both", [P, NS])
        stays = sb("stays", [P, NS])
        kept = sb("kept", [P, NS])
        kept_inv = sb("kept_inv", [P, NS])
        share = sb("share", [P, TC, SETS, PER_GROUP])
        group_share = sb("group_share", [P, TC, GROUPS])
        expert_weight = sb("expert_weight", [P, TC, GROUPS, PER_GROUP])
        far = sb("far", [P, NS, PER_GROUP])
        group_slot = sb("group_slot", [P, TC, GROUPS])
        slot = sb("slot", [P, TC, GROUPS, PER_GROUP])
        chosen = sb("chosen", [P, TC, EXPERTS], BF16)
        next_row = sb("next_row", [P, EXPERTS])
        place = sb("place", [P, TC, EXPERTS])
        place_of = sb("place_of", [P, SLOTS, TC, EXPERTS])
        weight_of = sb("weight_of", [P, SLOTS, TC, EXPERTS])
        place_in = sb("place_in", [P, SLOTS, TC])
        send_to = sb("send_to", [P, SLOTS, TC], I32)

        count = sb("count", [1, EXPERTS])
        count_i = sb("count_i", [1, EXPERTS], I32)
        tiles_i = sb("tiles_i", [1, EXPERTS], I32)
        tiles_of = sb("tiles_of", [1, EXPERTS])
        tiles_to = sb("tiles_to", [1, EXPERTS])
        passed = taps[0:1, :, :].rearrange("p t n -> p (t n)")[:, 0:TILES * EXPERTS].rearrange(
            "p (t e) -> p t e", e=EXPERTS)
        tile_expert = sb("tile_expert", [1, TILES])
        tiles_before = sb("tiles_before", [1, TILES])
        tile_in_region = sb("tile_in_region", [1, TILES])
        tile_region = sb("tile_region", [1, TILES])
        tile_row = sb("tile_row", [1, TILES], I32)
        tile_weights = sb("tile_weights", [1, TILES], I32)
        pad_start = sb("pad_start", [1, EXPERTS], I32)

        xs = sb("xs", [P, RING, REC])
        xsT = sb("xsT", [P, 2, P])
        gated = sb("gated", [P, 2, HID])
        hid = sb("hid", [P, 2, HID])
        hidT = sb("hidT", [P, HID])
        y = sb("y", [P, RING, D])
        add_to = sb("add_to", [P, RING], I32)

        ids_in = sem("ids_in")
        front_weights_in = sem("front_weights_in")
        w1_in, w3_in, w2_in = sem("w1_in"), sem("w3_in"), sem("w2_in")
        pool_step = sem("pool_step")
        constants_ready = sem("constants_ready")
        gathered = sem("gathered")
        gather_begun = sem("gather_begun")
        send_begun = sem("send_begun")
        embedded = sem("embedded")
        h_ready = sem("h_ready")
        stats_ready = sem("stats_ready")
        var_ready = sem("var_ready")
        std_ready = sem("std_ready")
        xn_ready = sem("xn_ready")
        xn_transposed = sem("xn_transposed")
        xT_ready = sem("xT_ready")
        q_done = sem("q_done")
        v_done = sem("v_done")
        qT_ready = sem("qT_ready")
        v_ready = sem("v_ready")
        scores_done = sem("scores_done")
        max_ready = sem("max_ready")
        probs_ready = sem("probs_ready")
        probs_transposed = sem("probs_transposed")
        pT_ready = sem("pT_ready")
        pv_done = sem("pv_done")
        h1_ready = sem("h1_ready")
        h1_stored = sem("h1_stored")
        x2_ready = sem("x2_ready")
        x2_transposed = sem("x2_transposed")
        x2T_ready = sem("x2T_ready")
        logits_done = sem("logits_done")
        shifted_ready = sem("shifted_ready")
        choice_ready = sem("choice_ready")
        chosen_ready = sem("chosen_ready")
        places_done = sem("places_done")
        rows_ready = sem("rows_ready")
        rows_sent = sem("rows_sent")
        vector_step = sem("vector_step")
        table_ready = sem("table_ready")
        zeros_stored = sem("zeros_stored")
        pads_stored = sem("pads_stored")
        xs_in = [sem(f"xs_in{n}") for n in range(RING)]
        xs_transposed = sem("xs_transposed")
        xsT_ready = sem("xsT_ready")
        gate_done = sem("gate_done")
        up_done = sem("up_done")
        gated_ready = sem("gated_ready")
        hid_ready = sem("hid_ready")
        low_transposed = sem("low_transposed")
        high_transposed = sem("high_transposed")
        hidT_low = sem("hidT_low")
        hidT_high = sem("hidT_high")
        down_done = sem("down_done")
        y_ready = sem("y_ready")
        y_free = sem("y_free")
        added = [sem(f"added{n}") for n in range(2)]
        sums_in = [sem(f"sums_in{n}") for n in range(CHUNKS)]
        out_ready = sem("out_ready")
        out_stored = sem("out_stored")

        sum_parts = [[h, xn], [h1, x2T[:, :].rearrange("p (t n) -> p t n", n=D)]]

        def older(c, b, n=BC):
            return c * n + max(b - 1, 0)

        block = ctx.enter_context(nc.Block())

        @block.sync
        def _(sp):
            sp.dma_start(ids_sb[:, :], ids).then_inc(ids_in, 16)
            for dst, src in (
                (wqk_sb[:, :], w_qk), (wvt_sb[:, :], w_v_t), (bv_sb[:, :], b_v.partition_broadcast(P)),
                (router_w[:, 0:EXPERTS], w_gate), (router_w[:, EXPERTS:], w_route),
                (router_b[:, 0:EXPERTS], b_gate.partition_broadcast(P)),
                (router_b[:, EXPERTS:], b_route.partition_broadcast(P)),
            ):
                sp.dma_start(dst, src).then_inc(front_weights_in, 16)
            sp.wait_ge(gathered, 16 * TC)
            for dst, src, landed in ((w1_sb, w1, w1_in), (w3_sb, w3, w3_in), (w2_sb, w2, w2_in)):
                sp.dma_start(dst[:, :], src).then_inc(landed, 16)
            sp.wait_ge(constants_ready, 1)
            sp.dma_start(sums[1].rearrange("(t p) n -> p t n", p=P),
                         zeros[:, :].unsqueeze(1).broadcast_to([P, TILES_IN + 1, D])).then_inc(zeros_stored, 16)
            sp.dma_start(sums[0][TOKENS:, :], zeros[:, :]).then_inc(zeros_stored, 16)
            sp.dma_start(sent[EXPERTS * REGION:, :].rearrange("(t p) n -> p t n", p=P),
                         pad_rows[:, :].unsqueeze(1).broadcast_to([P, SPARE, REC])).then_inc(pads_stored, 16)
            with sp.Fori(0, CHUNKS) as c:
                sp.wait_ge(h1_ready, c * BC + BC)
                sp.dma_start(sums[0][bass.ds(c * (TC * P), TC * P), :].rearrange("(t p) n -> p t n", p=P),
                             h1[:, :, :]).then_inc(h1_stored, 16)
            sp.wait_ge(table_ready, 1)
            for e in range(EXPERTS):
                start = sp.value_load(pad_start[0:1, e:e + 1], min_val=0, max_val=EXPERTS * REGION - P)
                sp.dma_start(sent[bass.ds(start, P), :], pad_rows[:, :]).then_inc(pads_stored, 16)
            sp.wait_ge(pads_stored, 16 * (EXPERTS + 1))
            sp.wait_ge(rows_sent, 16 * CHUNKS * TC * SLOTS)

            def load(t, ring):
                row = sp.value_load(tile_row[0:1, bass.ds(t, 1)], min_val=0, max_val=SENT_ROWS - P)
                sp.dma_start(xs[:, ring, :], sent[bass.ds(row, P), :]).then_inc(xs_in[ring], 16)

            for n in range(RING):
                load(n, n)
            with sp.Fori(0, AHEAD // RING) as i:
                for n in range(RING):
                    sp.wait_ge(hid_ready, i * RING + n + 1)
                    load(i * RING + n + RING, n)
            sp.wait_ge(added[0], 16 * TILES // 2)
            sp.wait_ge(added[1], 16 * TILES // 2)
            parts = [s.rearrange("(c p t) n -> c p t n", p=P, t=TC) for s in
                     (sums[0][0:TOKENS, :], sums[1][0:TOKENS, :])]
            out_parts = out.rearrange("b s n -> (b s) n").rearrange("(c p t) n -> c p t n", p=P, t=TC)
            for c in range(CHUNKS):
                if c >= 2:
                    sp.wait_ge(out_stored, 16 * (c - 1))
                for n in range(2):
                    sp.dma_start(sum_parts[c % 2][n][:, :, :], parts[n][c]).then_inc(sums_in[c], 16)
                if c >= 1:
                    sp.wait_ge(out_ready, c)
                    sp.dma_start(out_parts[c - 1], sum_parts[(c - 1) % 2][0][:, :, :]).then_inc(out_stored, 16)
            sp.wait_ge(out_ready, CHUNKS)
            sp.dma_start(out_parts[CHUNKS - 1], sum_parts[(CHUNKS - 1) % 2][0][:, :, :]).then_inc(out_stored, 16)
            sp.wait_ge(out_stored, 16 * CHUNKS)
            sp.wait_ge(zeros_stored, 32)
            sp.wait_ge(h1_stored, 16 * CHUNKS)

        @block.gpsimd
        def _(pool):
            steps = [0]

            def step(ins):
                steps[0] += 1
                ins.then_inc(pool_step, 1)

            def settle():
                pool.wait_ge(pool_step, steps[0])

            def gather(c):
                for t in range(TC):
                    nc.gpsimd.indirect_dma_start(
                        out=taps[:, t, :], out_offset=None, in_=embedding[:, :],
                        in_offset=bass.IndirectOffsetOnAxis(ap=gather_ids[:, t:t + 1], axis=0)
                    ).then_inc(gathered, 16)

            def send():
                for s in range(SLOTS):
                    for t in range(TC):
                        nc.gpsimd.indirect_dma_start(
                            out=sent[:, :], out_offset=bass.IndirectOffsetOnAxis(ap=send_to[:, s, t:t + 1], axis=0),
                            in_=rows[:, t, s, :], in_offset=None).then_inc(rows_sent, 16)

            pool.wait_ge(ids_in, 16)
            step(nc.gpsimd.tensor_copy(gather_ids[:, :], ids_sb[:, 0:TC]))
            settle()
            gather(0)
            for m, base, per_partition in ((ident, 0, -1), (from_before, -1, -1), (from_after, 1, -1),
                                           (last_to_first, P * (P - 1), -P), (first_to_last, -(P - 1), P)):
                step(nc.gpsimd.memset(m[:, :], 0.0))
                settle()
                step(nc.gpsimd.affine_select(out=m[:, :], in_=m[:, :], pattern=[[1, P]],
                                             compare_op=ALU.not_equal, fill=1.0, base=base,
                                             channel_multiplier=per_partition))
            step(nc.gpsimd.memset(ones[:, :], 1.0))
            settle()
            step(nc.gpsimd.affine_select(out=earlier[:, :], in_=ones[:, :], pattern=[[1, P]],
                                         compare_op=ALU.is_gt, fill=0.0, base=0, channel_multiplier=-1))
            step(nc.gpsimd.iota(position_bias[:, 0:P], pattern=[[1, P]], base=0, channel_multiplier=-1,
                                allow_small_or_imprecise_dtypes=True))
            step(nc.gpsimd.iota(position_bias[:, P:], pattern=[[1, 2 * P]], base=-P, channel_multiplier=-1,
                                allow_small_or_imprecise_dtypes=True))
            settle()
            step(nc.gpsimd.tensor_scalar(position_bias[:, :], position_bias[:, :], SLOPE, None, ALU.mult))
            settle()
            for cols, base in ((position_bias[:, 0:P], 0), (position_bias[:, P:], P)):
                step(nc.gpsimd.affine_select(out=cols, in_=cols, pattern=[[-1, cols.shape[1]]],
                                             compare_op=ALU.is_ge, fill=MASKED, base=base, channel_multiplier=1))
            step(nc.gpsimd.memset(eps[:, :], EPS))
            step(nc.gpsimd.memset(zeros[:, :], 0.0))
            step(nc.gpsimd.memset(pad_rows[:, 0:REC - 1], 0.0))
            step(nc.gpsimd.iota(pad_rows[:, REC - 1:], pattern=[[0, 1]], base=TOKENS, channel_multiplier=1,
                                allow_small_or_imprecise_dtypes=True))
            step(nc.gpsimd.iota(token_number[:, :], pattern=[[P, TILES_IN]], base=0, channel_multiplier=1,
                                allow_small_or_imprecise_dtypes=True))
            for m in (region_start, next_row):
                step(nc.gpsimd.iota(m[:, :], pattern=[[REGION, EXPERTS]], base=0, channel_multiplier=0,
                                    allow_small_or_imprecise_dtypes=True))
            step(nc.gpsimd.iota(tile_number[:, :], pattern=[[1, TILES]], base=0, channel_multiplier=0,
                                allow_small_or_imprecise_dtypes=True))
            step(nc.gpsimd.memset(ones_row[:, :], 1.0))
            settle()
            pool.sem_inc(constants_ready, 1)
            before = steps[0]

            with pool.Fori(0, CHUNKS - 1) as c:
                pool.wait_ge(embedded, c * BC + BC)
                pool.tensor_copy(gather_ids[:, :], ids_sb[:, bass.ds(c * TC + TC, TC)]).then_inc(pool_step, 1)
                pool.wait_ge(pool_step, c + (before + 1))
                pool.sem_inc(gather_begun, 1)
                gather(c + 1)
                pool.wait_ge(rows_ready, c + 1)
                pool.sem_inc(send_begun, 1)
                send()
            pool.wait_ge(rows_ready, CHUNKS)
            send()

            pool.sem_inc(y_free, 2)
            pool.wait_ge(zeros_stored, 32)
            pool.wait_ge(h1_stored, 16 * CHUNKS)
            with pool.Fori(0, TILES // RING) as i:
                for n in range(RING):
                    pool.wait_ge(y_ready, i * RING + n + 1)
                    pool.wait_ge(added[n % 2], i * (16 * RING // 2) + 16 * (n // 2))
                    pool.sem_inc(y_free, 1)
                    nc.gpsimd.indirect_dma_start(
                        out=sums[n % 2][:, :], out_offset=bass.IndirectOffsetOnAxis(ap=add_to[:, n:n + 1], axis=0),
                        in_=y[:, n, :], in_offset=None, compute_op=ALU.add).then_inc(added[n % 2], 16)

        @block.scalar
        def _(act):
            act.wait_ge(constants_ready, 1)

            def copy_xT(c, b):
                act.wait_ge(xn_transposed, c * BC + b + 1)
                act.wait_ge(scores_done, older(c, b))
                nc.scalar.copy(xT[:, b % 2, :], bank[2][:, 0:SEQ]).then_inc(xT_ready, 1)

            def copy_qT(c, b):
                act.wait_ge(q_done, c * BC + b + 1)
                nc.scalar.copy(qT[:, b % 2, :], bank[3][:, 0:SEQ]).then_inc(qT_ready, 1)

            def exponentials(c, b):
                act.wait_ge(max_ready, c * BC + b + 1)
                act.wait_ge(probs_transposed, older(c, b))
                act.wait_ge(h1_ready, older(c, b))
                nc.scalar.activation(probs[:, b % 2, 0:P], scores[:, b % 2, 0:P], ACT.Exp,
                                     bias=neg_max[:, b % 2, 0:1], accum_out=row_sum[:, b % 2, 0:1])
                nc.scalar.activation(probs[:, b % 2, P:], scores[:, b % 2, P:], ACT.Exp,
                                     bias=neg_max[:, b % 2, 1:2], accum_out=row_sum[:, b % 2, 1:2]
                                     ).then_inc(probs_ready, 1)

            def copy_pT(c, b):
                act.wait_ge(probs_transposed, c * BC + b + 1)
                act.wait_ge(pv_done, older(c, b))
                nc.scalar.copy(pT[:, b % 2, :], bank[6][:, 0:3 * P]).then_inc(pT_ready, 1)

            with act.Fori(0, CHUNKS) as c:
                act.wait_ge(h1_ready, c * BC)
                for b in range(BC):
                    act.wait_ge(embedded, c * BC + b + 1)
                    nc.scalar.copy(h[:, 2 * b:2 * b + 2, :].rearrange("p t n -> p (t n)"),
                                   bank[b % 2][:, 0:SEQ]).then_inc(h_ready, 1)
                act.wait_ge(var_ready, c * 2 + 1)
                nc.scalar.activation(std[:, :], var[:, :], ACT.Sqrt, bias=eps[:, 0:1],
                                     scale=0.25).then_inc(std_ready, 1)
                copy_xT(c, 0)
                copy_qT(c, 0)
                for b in range(BC):
                    if b + 1 < BC:
                        copy_xT(c, b + 1)
                        copy_qT(c, b + 1)
                    exponentials(c, b)
                    copy_pT(c, b)
                act.wait_ge(var_ready, c * 2 + 2)
                nc.scalar.activation(std2[:, :], var[:, :], ACT.Sqrt, bias=eps[:, 0:1],
                                     scale=0.25).then_inc(std_ready, 1)
                for n in range(2):
                    act.wait_ge(x2_transposed, c * 2 + n + 1)
                    act.wait_ge(logits_done, c)
                    nc.scalar.copy(x2T[:, n * 512:(n + 1) * 512], bank[n][:, :]).then_inc(x2T_ready, 1)
                act.wait_ge(shifted_ready, c + 1)
                nc.scalar.activation(choice[:, :, :], shifted[:, :, :], ACT.Exp).then_inc(choice_ready, 1)

            def copy_xsT(t, ring):
                act.wait_ge(xs_transposed, t + 1)
                nc.scalar.copy(xsT[:, ring % 2, :], bank[6][:, 0:P]).then_inc(xsT_ready, 1)

            def silu(t, ring):
                act.wait_ge(gate_done, t + 1)
                nc.scalar.activation(gated[:, ring % 2, :], bank[ring % 2][:, :], ACT.Silu).then_inc(gated_ready, 1)

            def step(j, n, rest):
                act.wait_ge(low_transposed, j + 1)
                act.wait_ge(down_done, j)
                nc.scalar.copy(hidT[:, 0:HID // 2], bank[4][:, 0:HID // 2]).then_inc(hidT_low, 1)
                if rest > 1:
                    act.wait_ge(hid_ready, j)
                    silu(j + 1, n + 1)
                if rest > 2:
                    act.wait_ge(up_done, j + 1)
                    copy_xsT(j + 2, n + 2)

            copy_xsT(0, 0)
            copy_xsT(1, 1)
            silu(0, 0)
            with act.Fori(0, AHEAD // RING) as i:
                for n in range(RING):
                    step(i * RING + n, n, RING)
            for n in range(RING):
                step(AHEAD + n, n, RING - n)

        @block.vector
        def _(dve):
            steps = [0]
            before = [0]

            def link(ins):
                steps[0] += 1
                ins.then_inc(vector_step, 1)
                dve.wait_ge(vector_step, before[0] + steps[0])

            def cells(ap, shape):
                return ap.broadcast_to(shape)

            tt, ts, stt = nc.vector.tensor_tensor, nc.vector.tensor_scalar, nc.vector.scalar_tensor_tensor

            def values_and_scores(c, b):
                dve.wait_ge(v_done, c * BC + b + 1)
                dve.wait_ge(pv_done, older(c, b))
                tt(v[:, b % 2, :].rearrange("p (t n) -> p t n", t=2),
                   bank[5][:, 0:SEQ].rearrange("p (t n) -> p t n", t=2),
                   cells(bv_sb[:, :].unsqueeze(1), [P, 2, D]), ALU.add).then_inc(v_ready, 1)
                dve.wait_ge(scores_done, c * BC + b + 1)
                dve.wait_ge(probs_ready, older(c, b))
                link(stt(scores[:, b % 2, :], bank[4][:, 0:3 * P], SCALE, position_bias[:, :],
                         ALU.mult, ALU.add))
                nc.vector.tensor_reduce(neg_max[:, b % 2, 0:1], scores[:, b % 2, 0:P], AX.X, ALU.max, negate=True)
                nc.vector.tensor_reduce(neg_max[:, b % 2, 1:2], scores[:, b % 2, P:], AX.X, ALU.max,
                                        negate=True).then_inc(max_ready, 1)

            def residual(c, b):
                if b == 0:
                    dve.wait_ge(h1_stored, c * 16)
                dve.wait_ge(probs_ready, c * BC + b + 1)
                link(nc.vector.reciprocal(row_inv[:, b % 2, :], row_sum[:, b % 2, :]))
                dve.wait_ge(pv_done, c * BC + b + 1)
                for t in range(2):
                    last = stt(h1[:, 2 * b + t, :], bank[7][:, t * D:(t + 1) * D], row_inv[:, b % 2, t:t + 1],
                               h[:, 2 * b + t, :], ALU.mult, ALU.add)
                link(last)
                for t in range(2):
                    last = nc.vector.bn_stats(stats2[:, 2 * b + t, :], h1[:, 2 * b + t, :])
                last.then_inc(h1_ready, 1)

            def moments(of, ready_before, count):
                dve.wait_ge(ready_before, count)
                summed, apart, squares, square = (half_sums[:, n, :] for n in range(4))
                tt(summed, of[:, :, 1], of[:, :, 4], ALU.add)
                tt(apart, of[:, :, 1], of[:, :, 4], ALU.subtract)
                link(tt(squares, of[:, :, 2], of[:, :, 5], ALU.add))
                ts(mean[:, :], summed, 0.5, None, ALU.mult)
                link(tt(square, apart, apart, ALU.mult))
                stt(var[:, :], squares, 4.0 / D, square, ALU.mult, ALU.add).then_inc(var_ready, 1)

            def route(c):
                all4 = [P, NS, PER_GROUP]
                dve.wait_ge(logits_done, c + 1)
                link(tt(logits[:, :, :].rearrange("p (t g) e -> p t (g e)", g=SETS),
                        bank[3][:, 0:TC * SETS * PER_GROUP].rearrange("p (t n) -> p t n", t=TC),
                        cells(router_b[:, :].unsqueeze(1), [P, TC, SETS * PER_GROUP]), ALU.add))
                link(nc.vector.tensor_reduce(set_max[:, :], logits[:, :, :], AX.X, ALU.max))
                tt(shifted[:, :, :], logits[:, :, :], cells(set_max[:, :].unsqueeze(2), all4),
                   ALU.subtract).then_inc(shifted_ready, 1)
                dve.wait_ge(choice_ready, c + 1)
                link(nc.vector.tensor_reduce(set_sum[:, :], choice[:, :, :], AX.X, ALU.add))
                link(nc.vector.reciprocal(set_inv[:, :], set_sum[:, :]))
                link(tt(choice[:, :, :], choice[:, :, :], cells(set_inv[:, :].unsqueeze(2), all4), ALU.mult))
                for i, at in ((0, 0), (1, 3), (2, 5)):
                    n = PER_GROUP - 1 - i
                    last = tt(beats[:, :, at:at + n], cells(choice[:, :, i:i + 1], [P, NS, n]),
                              choice[:, :, i + 1:], ALU.is_ge)
                link(last)

                def pair(n):
                    return beats[:, :, n:n + 1]

                tt(part[:, :, 0:1], pair(0), pair(1), ALU.add)
                tt(part[:, :, 1:2], pair(3), pair(4), ALU.add)
                tt(part[:, :, 2:3], pair(1), pair(3), ALU.add)
                link(tt(part[:, :, 3:4], pair(2), pair(4), ALU.add))
                tt(rank[:, :, 0:1], part[:, :, 0:1], pair(2), ALU.add)
                stt(rank[:, :, 1:2], pair(0), 2.0, part[:, :, 1:2], ALU.add, ALU.subtract)
                stt(rank[:, :, 2:3], part[:, :, 2:3], 1.0, pair(5), ALU.add, ALU.subtract)
                link(tt(rank[:, :, 3:4], part[:, :, 3:4], pair(5), ALU.add))
                link(ts(rank[:, :, 0:1], rank[:, :, 0:1], -1.0, 3.0, ALU.mult, ALU.add))
                ts(far[:, :, :], rank[:, :, :], 2.0, 8.0, ALU.is_ge, ALU.mult)
                ts(is_first[:, :, :], rank[:, :, :], 0.0, None, ALU.is_equal)
                link(ts(is_second[:, :, :], rank[:, :, :], 1.0, None, ALU.is_equal))
                far_of = far[:, :, :].rearrange("p (t g) e -> p t g e", g=SETS)
                rank_of = rank[:, :, :].rearrange("p (t g) e -> p t g e", g=SETS)
                stt(group_slot[:, :, :], rank_of[:, :, GROUPS, :], 2.0, far_of[:, :, GROUPS, :], ALU.mult, ALU.add)
                link(tt(slot[:, :, :, :], rank_of[:, :, 0:GROUPS, :], far_of[:, :, 0:GROUPS, :], ALU.add))
                link(tt(slot[:, :, :, :], slot[:, :, :, :],
                        cells(group_slot[:, :, :].unsqueeze(3), [P, TC, GROUPS, PER_GROUP]), ALU.add))
                slots = slot[:, :, :, :].rearrange("p t g e -> p t (g e)")
                ts(chosen[:, :, :], slots, float(SLOTS), None, ALU.is_lt).then_inc(chosen_ready, 1)
                tt(part[:, :, :], choice[:, :, :], is_first[:, :, :], ALU.mult)
                link(tt(shifted[:, :, :], choice[:, :, :], is_second[:, :, :], ALU.mult))
                nc.vector.tensor_reduce(p_first[:, :], part[:, :, :], AX.X, ALU.add)
                link(nc.vector.tensor_reduce(p_second[:, :], shifted[:, :, :], AX.X, ALU.add))
                link(tt(both[:, :], p_first[:, :], p_second[:, :], ALU.add))
                link(ts(stays[:, :], both[:, :], KEEP, None, ALU.is_le))
                link(tt(kept[:, :], p_second[:, :], stays[:, :], ALU.mult))
                tt(shifted[:, :, :], shifted[:, :, :], cells(stays[:, :].unsqueeze(2), all4), ALU.mult)
                link(stt(kept[:, :], kept[:, :], 1.0, p_first[:, :], ALU.mult, ALU.add))
                link(ts(kept[:, :], kept[:, :], 1e-9, None, ALU.add))
                tt(part[:, :, :], part[:, :, :], shifted[:, :, :], ALU.add)
                link(nc.vector.reciprocal(kept_inv[:, :], kept[:, :]))
                shares = share[:, :, :, :].rearrange("p t g e -> p (t g) e")
                link(tt(shares, part[:, :, :], cells(kept_inv[:, :].unsqueeze(2), all4), ALU.mult))
                link(ts(group_share[:, :, :], share[:, :, GROUPS, :], float(GROUPS) ** -0.5, None, ALU.mult))
                link(tt(expert_weight[:, :, :, :], share[:, :, 0:GROUPS, :],
                        cells(group_share[:, :, :].unsqueeze(3), [P, TC, GROUPS, PER_GROUP]), ALU.mult))
                weights = expert_weight[:, :, :, :].rearrange("p t g e -> p t (g e)")
                for s in range(SLOTS):
                    stt(weight_of[:, s], slots, float(s), weights, ALU.is_equal, ALU.mult)
                dve.wait_ge(places_done, c + 1)
                link(tt(place[:, :, :], bank[6][:, 0:TC * EXPERTS].rearrange("p (t e) -> p t e", t=TC),
                        cells(next_row[:, :].unsqueeze(1), [P, TC, EXPERTS]), ALU.add))
                tt(next_row[:, :], next_row[:, :], bank[6][:, TC * EXPERTS:(TC + 1) * EXPERTS], ALU.add)
                for s in range(SLOTS):
                    last = stt(place_of[:, s], slots, float(s), place[:, :, :], ALU.is_equal, ALU.mult)
                link(last)
                link(nc.vector.tensor_reduce(place_in[:, :, :], place_of[:, :, :, :], AX.X, ALU.add))
                nc.vector.tensor_copy(send_to[:, :, :], place_in[:, :, :])
                nc.vector.tensor_reduce(rows[:, :, :, D].rearrange("p t s -> p s t"), weight_of[:, :, :, :],
                                        AX.X, ALU.add).then_inc(rows_ready, 1)

            dve.wait_ge(constants_ready, 1)
            dve.wait_ge(front_weights_in, 16 * 7)
            with dve.Fori(0, CHUNKS) as c:
                before[0] = c * VECTOR_PER_CHUNK + VECTOR_BEFORE
                for b in range(BC):
                    dve.wait_ge(h_ready, c * BC + b + 1)
                    for t in (2 * b, 2 * b + 1):
                        last = nc.vector.bn_stats(stats[:, t, :], h[:, t, :])
                    last.then_inc(stats_ready, 1)
                moments(stats, stats_ready, c * BC + BC)
                dve.wait_ge(std_ready, c * 2 + 1)
                link(nc.vector.reciprocal(rstd[:, :], std[:, :]))
                dve.wait_ge(xn_transposed, c * BC)
                for t in range(TC):
                    last = ts(xn[:, t, :], h[:, t, :], mean[:, t:t + 1], rstd[:, t:t + 1],
                              ALU.subtract, ALU.mult)
                    if t % 2:
                        last.then_inc(xn_ready, 1)
                values_and_scores(c, 0)
                for b in range(BC):
                    if b + 1 < BC:
                        values_and_scores(c, b + 1)
                    residual(c, b)
                moments(stats2, h1_ready, c * BC + BC)
                dve.wait_ge(std_ready, c * 2 + 2)
                link(nc.vector.reciprocal(rstd2[:, :], std2[:, :]))
                dve.wait_ge(rows_sent, c * (16 * TC * SLOTS))
                for t in range(TC):
                    last = ts(rows[:, t, :, 0:D], cells(h1[:, t, :].unsqueeze(1), [P, SLOTS, D]),
                              mean[:, t:t + 1], rstd2[:, t:t + 1], ALU.subtract, ALU.mult)
                    if t % 4 == 3:
                        last.then_inc(x2_ready, 1)
                nc.vector.tensor_copy(rows[:, :, :, D + 1],
                                      cells(token_number[:, bass.ds(c * TC, TC)].unsqueeze(2), [P, TC, SLOTS]))
                route(c)
            assert steps[0] == VECTOR_PER_CHUNK, steps[0]
            before[0], steps[0] = VECTOR_BEFORE + CHUNKS * VECTOR_PER_CHUNK, 0

            by_tile = [1, TILES, EXPERTS]
            nc.vector.tensor_copy(pad_start[:, :], next_row[0:1, :])
            link(tt(count[:, :], next_row[0:1, :], region_start[0:1, :], ALU.subtract))
            link(ts(count_i[:, :], count[:, :], float(P - 1), None, ALU.add))
            link(ts(tiles_i[:, :], count_i[:, :], P.bit_length() - 1, None, ALU.logical_shift_right))
            link(nc.vector.tensor_copy(tiles_of[:, :], tiles_i[:, :]))
            link(nc.vector.tensor_tensor_scan(tiles_to[:, :], ones_row[:, :], tiles_of[:, :], 0.0,
                                              ALU.mult, ALU.add))
            link(tt(passed[:, :, :], cells(tiles_to[:, :].unsqueeze(1), by_tile),
                    cells(tile_number[:, :].unsqueeze(2), by_tile), ALU.is_le))
            link(nc.vector.tensor_reduce(tile_expert[:, :], passed[:, :, :], AX.X, ALU.add))
            link(tt(passed[:, :, :], passed[:, :, :], cells(tiles_of[:, :].unsqueeze(1), by_tile), ALU.mult))
            link(nc.vector.tensor_reduce(tiles_before[:, :], passed[:, :, :], AX.X, ALU.add))
            tt(tile_in_region[:, :], tile_number[:, :], tiles_before[:, :], ALU.subtract)
            link(ts(tile_region[:, :], tile_expert[:, :], float(REGION), None, ALU.mult))
            stt(tile_row[:, :], tile_in_region[:, :], float(P), tile_region[:, :], ALU.mult, ALU.add)
            ts(tile_weights[:, :], tile_expert[:, :], float(EXPERTS - 1), float(HID), ALU.min,
               ALU.mult).then_inc(table_ready, 1)

            def hidden(t, n):
                dve.wait_ge(xs_in[n % RING], (t + 1 - (n % RING)) * (16 // RING) + (16 - 16 // RING))
                dve.wait_ge(y_free, t + 1)
                nc.vector.tensor_copy(add_to[:, n % RING:n % RING + 1], xs[:, n % RING, D + 1:D + 2])
                dve.wait_ge(up_done, t + 1)
                dve.wait_ge(gated_ready, t + 1)
                stt(hid[:, n % 2, :], gated[:, n % 2, :], xs[:, n % RING, D:D + 1], bank[2 + n % 2][:, :],
                    ALU.mult, ALU.mult).then_inc(hid_ready, 1)

            def step(j, n, rest):
                dve.wait_ge(high_transposed, j + 1)
                dve.wait_ge(down_done, j)
                nc.vector.tensor_copy(hidT[:, HID // 2:], bank[5][:, 0:HID // 2]).then_inc(hidT_high, 1)
                if rest > 1:
                    hidden(j + 1, n + 1)
                dve.wait_ge(down_done, j + 1)
                nc.vector.tensor_copy(y[:, n, :], bank[7][:, 0:D]).then_inc(y_ready, 1)

            hidden(0, 0)
            with dve.Fori(0, AHEAD // RING) as i:
                for n in range(RING):
                    step(i * RING + n, n, RING)
            for n in range(RING):
                step(AHEAD + n, n, RING - n)

            for c in range(CHUNKS):
                dve.wait_ge(sums_in[c], 32)
                first, second = sum_parts[c % 2]
                tt(first[:, :, :], first[:, :, :], second[:, :, :], ALU.add).then_inc(out_ready, 1)

        @block.tensor
        def _(pe):
            mm = nc.tensor.matmul
            pe.wait_ge(constants_ready, 1)
            pe.wait_ge(front_weights_in, 16 * 7)

            def embed(c, b):
                to = bank[b % 2]
                whole = to[:, 0:SEQ].rearrange("p (t n) -> p t n", t=2)
                first, second = to[:, 0:D], to[:, D:SEQ]
                pair = taps[:, 2 * b:2 * b + 2, :]
                mm(whole, from_before[:, :], pair[:, :, 0:D], start=True, stop=False)
                mm(second, last_to_first[:, :], taps[:, 2 * b, 0:D], start=False, stop=False)
                mm(whole, ident[:, :], pair[:, :, D:2 * D], start=False, stop=False)
                mm(whole, from_after[:, :], pair[:, :, 2 * D:3 * D], start=False, stop=False)
                mm(first, first_to_last[:, :], taps[:, 2 * b + 1, 2 * D:3 * D],
                   start=False, stop=True).then_inc(embedded, 1)

            def to_scores(c, b):
                pe.wait_ge(xn_ready, c * BC + b + 1)
                pe.wait_ge(xT_ready, c * BC + b)
                for t in range(2):
                    last = nc.tensor.transpose(bank[2][:, t * P:(t + 1) * P], xn[:, 2 * b + t, :], ident[:, :])
                last.then_inc(xn_transposed, 1)
                pe.wait_ge(xT_ready, c * BC + b + 1)
                pe.wait_ge(qT_ready, c * BC + b)
                if b == 0:
                    pe.wait_ge(shifted_ready, c)
                mm(bank[3][:, 0:SEQ], wqk_sb[:, :], xT[:, b % 2, :], start=True, stop=True).then_inc(q_done, 1)
                pe.wait_ge(v_ready, c * BC + b)
                for t in range(2):
                    last = mm(bank[5][:, t * D:(t + 1) * D], xT[:, b % 2, t * P:(t + 1) * P],
                              wvt_sb[:, :], start=True, stop=True)
                last.then_inc(v_done, 1)
                pe.wait_ge(qT_ready, c * BC + b + 1)
                pe.wait_ge(max_ready, c * BC + b)
                mm(bank[4][:, 0:P], qT[:, b % 2, 0:P], xT[:, b % 2, 0:P], start=True, stop=True)
                mm(bank[4][:, P:3 * P], qT[:, b % 2, P:], xT[:, b % 2, :],
                   start=True, stop=True).then_inc(scores_done, 1)

            def attend(c, b):
                pe.wait_ge(probs_ready, c * BC + b + 1)
                pe.wait_ge(pT_ready, c * BC + b)
                if b == 0:
                    pe.wait_ge(rows_ready, c)
                for n in range(3):
                    last = nc.tensor.transpose(bank[6][:, n * P:(n + 1) * P], probs[:, b % 2, n * P:(n + 1) * P],
                                               ident[:, :])
                last.then_inc(probs_transposed, 1)
                pe.wait_ge(pT_ready, c * BC + b + 1)
                pe.wait_ge(v_ready, c * BC + b + 1)
                pe.wait_ge(h1_ready, c * BC + b)
                mm(bank[7][:, 0:D], pT[:, b % 2, 0:P], v[:, b % 2, 0:D], start=True, stop=True)
                mm(bank[7][:, D:SEQ], pT[:, b % 2, P:2 * P], v[:, b % 2, 0:D], start=True, stop=False)
                mm(bank[7][:, D:SEQ], pT[:, b % 2, 2 * P:], v[:, b % 2, D:],
                   start=False, stop=True).then_inc(pv_done, 1)

            def route(c):
                for n in range(2):
                    pe.wait_ge(x2_ready, c * 2 + n + 1)
                    pe.wait_ge(h_ready, c * BC + BC)
                    for t in range(4):
                        last = nc.tensor.transpose(bank[n][:, t * P:(t + 1) * P], rows[:, 4 * n + t, 0, 0:D],
                                                   ident[:, :])
                    last.then_inc(x2_transposed, 1)
                pe.wait_ge(qT_ready, c * BC + BC)
                wide = SETS * PER_GROUP
                for t in range(TC):
                    if t % 4 == 0:
                        pe.wait_ge(x2T_ready, c * 2 + t // 4 + 1)
                    last = mm(bank[3][:, t * wide:(t + 1) * wide], x2T[:, t * P:(t + 1) * P], router_w[:, :],
                              start=True, stop=True)
                last.then_inc(logits_done, 1)
                pe.wait_ge(chosen_ready, c + 1)
                pe.wait_ge(pT_ready, c * BC + BC)
                n = TC * EXPERTS
                mm(bank[6][:, 0:n], earlier[:, :], chosen[:, :, :].rearrange("p t e -> p (t e)"),
                   start=True, stop=False)
                for t in range(TC - 1):
                    mm(bank[6][:, (t + 1) * EXPERTS:n].rearrange("p (t e) -> p t e", e=EXPERTS), ones[:, :],
                       chosen[:, t:t + 1, :].broadcast_to([P, TC - 1 - t, EXPERTS]),
                       start=False, stop=(t == TC - 2))
                for t in range(TC):
                    last = mm(bank[6][:, n:n + EXPERTS], ones[:, :], chosen[:, t, :], start=(t == 0),
                              stop=(t == TC - 1))
                last.then_inc(places_done, 1)

            with pe.Fori(0, CHUNKS) as c:
                pe.wait_ge(gathered, c * (16 * TC) + 16 * TC)
                pe.wait_ge(x2T_ready, c * 2)
                for b in range(BC):
                    if b >= 2:
                        pe.wait_ge(h_ready, c * BC + b - 1)
                    embed(c, b)
                to_scores(c, 0)
                for b in range(BC):
                    if b + 1 < BC:
                        to_scores(c, b + 1)
                    attend(c, b)
                route(c)

            pe.wait_ge(table_ready, 1)
            pe.wait_ge(w1_in, 16)
            pe.wait_ge(w3_in, 16)
            pe.wait_ge(w2_in, 16)

            most = (EXPERTS - 1) * HID
            carried = [pe.alloc_register(f"weights_at{n}") for n in range(2)]

            def weights_at(t):
                return pe.value_load(tile_weights[0:1, bass.ds(t, 1)], min_val=0, max_val=most)

            def carry(t, n):
                pe.reg_load(carried[n], tile_weights[0:1, bass.ds(t, 1)])

            def transpose_xs(t, n):
                pe.wait_ge(xs_in[n % RING], (t + 1 - (n % RING)) * (16 // RING) + (16 - 16 // RING))
                nc.tensor.transpose(bank[6][:, 0:P], xs[:, n % RING, 0:D],
                                    ident[:, :]).then_inc(xs_transposed, 1)

            def gate(t, n, at):
                pe.wait_ge(xsT_ready, t + 1)
                mm(bank[n % 2][:, :], xsT[:, n % 2, :], w1_sb[:, bass.ds(at, HID)],
                   start=True, stop=True).then_inc(gate_done, 1)

            def up(n, at):
                mm(bank[2 + n % 2][:, :], xsT[:, n % 2, :], w3_sb[:, bass.ds(at, HID)],
                   start=True, stop=True).then_inc(up_done, 1)

            def step(j, n, at, rest):
                if rest > 1:
                    gate(j + 1, n + 1, at[n + 1])
                pe.wait_ge(hid_ready, j + 1)
                for half, transposed in ((0, low_transposed), (1, high_transposed)):
                    for k in range(HK // 2):
                        at_k = (half * HK // 2 + k) * P
                        last = nc.tensor.transpose(bank[4 + half][:, k * P:(k + 1) * P],
                                                   hid[:, n % 2, at_k:at_k + P], ident[:, :])
                    last.then_inc(transposed, 1)
                if rest > 1:
                    up(n + 1, at[n + 1])
                if rest > 2:
                    transpose_xs(j + 2, n + 2)
                    if n + 2 <= RING:
                        at.append(weights_at(j + 2))
                    if n + 2 >= RING:
                        carry(j + 2, n + 2 - RING)
                pe.wait_ge(hidT_low, j + 1)
                pe.wait_ge(hidT_high, j + 1)
                for k in range(HK):
                    last = mm(bank[7][:, 0:D], hidT[:, k * P:(k + 1) * P],
                              w2_sb[:, bass.ds(at[n] + k * D, D)], start=(k == 0), stop=(k == HK - 1))
                last.then_inc(down_done, 1)

            transpose_xs(0, 0)
            pe.wait_ge(xsT_ready, 1)
            transpose_xs(1, 1)
            carry(0, 0)
            carry(1, 1)
            first_at = weights_at(0)
            gate(0, 0, first_at)
            up(0, first_at)

            def taken():
                return [pe.snap(r, min_val=0, max_val=most) for r in carried]

            with pe.Fori(0, AHEAD // RING) as i:
                at = taken()
                for n in range(RING):
                    step(i * RING + n, n, at, RING)
            at = taken()
            for n in range(RING):
                step(AHEAD + n, n, at, RING - n)


def kernel(x, L0_tok_conv_w, L0_attn_W_qk, L0_attn_W_v, L0_attn_b_v, L0_ffn_Wr, L0_ffn_br, L0_ffn_Wgate,
           L0_ffn_bgate, L0_ffn_W1, L0_ffn_W3, L0_ffn_W2):
    import numpy as np
    import concourse.bacc as bacc
    from concourse.bass_utils import run_bass_kernel_spmd

    lay = np.ascontiguousarray
    arrays = {
        "ids": lay(np.asarray(x).reshape(TILES_IN, P).T),
        "embedding": lay(np.asarray(L0_tok_conv_w).transpose(1, 2, 0).reshape(VOCAB, TAPS * D)),
        "w_qk": lay(L0_attn_W_qk),
        "w_v_t": lay(np.asarray(L0_attn_W_v).T),
        "b_v": lay(L0_attn_b_v),
        "w_route": lay(L0_ffn_Wr),
        "w_gate": lay(np.asarray(L0_ffn_Wgate).transpose(1, 0, 2).reshape(D, EXPERTS)),
        "b_route": lay(L0_ffn_br),
        "b_gate": lay(np.asarray(L0_ffn_bgate).reshape(EXPERTS)),
        "w1": lay(np.asarray(L0_ffn_W1).transpose(1, 0, 2).reshape(D, EXPERTS * HID)),
        "w3": lay(np.asarray(L0_ffn_W3).transpose(1, 0, 2).reshape(D, EXPERTS * HID)),
        "w2": lay(np.asarray(L0_ffn_W2).reshape(EXPERTS, HK, P, D).transpose(2, 0, 1, 3).reshape(P, -1)),
    }
    nc = bacc.Bacc("TRN2", target_bir_lowering=False, num_devices=1)
    args = [nc.dram_tensor(name, a.shape, mybir.dt.from_np(a.dtype), kind="ExternalInput").ap()
            for name, a in arrays.items()]
    out = nc.dram_tensor("out", [BATCHES, SEQ, D], F32, kind="ExternalOutput").ap()
    tower_kernel(nc, *args, out)
    return run_bass_kernel_spmd(nc, [arrays], core_ids=[0]).results[0]["out"]
```

```python
from contextlib import ExitStack

import concourse.bass as bass
from concourse import mybir

F32 = mybir.dt.float32
F32R = mybir.dt.float32r
BF16 = mybir.dt.bfloat16
I32 = mybir.dt.int32
ALU = mybir.AluOpType
ACT = mybir.ActivationFunctionType
AX = mybir.AxisListType

P = 128
D = 128
TAPS = 3
VOCAB = 8000
BATCHES, SEQ = 16, 256
TOKENS = BATCHES * SEQ
TILES_IN = TOKENS // P
CHUNKS = 8
TC = TILES_IN // CHUNKS
BC = BATCHES // CHUNKS
GROUPS, PER_GROUP = 4, 4
EXPERTS = GROUPS * PER_GROUP
SETS = GROUPS + 1
SLOTS = 4
HID = 512
HK = HID // P
KEEP = 0.9
EPS = 1e-5
SCALE = float(D) ** -0.5
SLOPE = 0.5
MASKED = -3.0e38

REC = D + EXPERTS + 1
REGION = TOKENS + P
TILES = 144
SPARE = TILES - TOKENS * SLOTS // P
SENT_ROWS = EXPERTS * REGION + SPARE * P
RING = 4
AHEAD = TILES - RING

PART = EXPERTS * HID // CHUNKS
PIECES = 2 * PART // 512
LAST_CHUNKS = 8
FRONT = (CHUNKS - 2) // 2
VECTOR_PER_PASS = 2 * (26 + 3 * BC)


def tower_kernel(nc, ids, embedding, w_qk, w_v_t, b_v, w_route, w_gate, b_route, b_gate, w1, w3, w2, out):
    ctx = ExitStack()
    with ctx:
        def sb(name, shape, dt=F32):
            return ctx.enter_context(nc.sbuf_tensor(name, shape, dt))

        def sem(name):
            return ctx.enter_context(nc.semaphore(name))

        bank = [ctx.enter_context(nc.psum_tensor(f"bank{n}", [P, 512], F32)) for n in range(8)]

        sent = nc.dram_tensor("sent", [SENT_ROWS, REC], F32, kind="Internal").ap()
        sums = [nc.dram_tensor(f"sums{n}", [TOKENS + P, D], F32, kind="Internal").ap() for n in range(2)]

        START = -(-nc.sbuf_base // 32) * 32
        WEIGHTS = EXPERTS * HID
        sb("weights_space", [P, 4 * WEIGHTS + TC * P])

        def within(name, floats_in, shape, dt=F32):
            return nc.alloc_sbuf_tensor_at(name, shape, dt, offset=START + 4 * floats_in)

        w_high = [within(f"w{n}_high", i * WEIGHTS, [P, WEIGHTS], F32R) for i, n in enumerate((1, 3))]
        w_low = [within(f"w{n}_low", (2 + i) * WEIGHTS, [P, WEIGHTS], F32R) for i, n in enumerate((1, 3))]
        w_raw = [within(f"w{n}_raw", (2 + i) * WEIGHTS, [P, WEIGHTS]) for i, n in enumerate((1, 3))]
        LATE_FROM = EXPERTS * HID * (CHUNKS - 2) // CHUNKS
        late = [i * WEIGHTS + LATE_FROM for i in range(2)]
        assert 2 * 2 * TC * D == WEIGHTS - LATE_FROM and TC * D + 3 * 2 * SEQ == WEIGHTS - LATE_FROM

        ident = sb("ident", [P, P])
        from_before = sb("from_before", [P, P])
        from_after = sb("from_after", [P, P])
        last_to_first = sb("last_to_first", [P, P])
        first_to_last = sb("first_to_last", [P, P])
        earlier = sb("earlier", [P, P], BF16)
        ones = sb("ones", [P, P], BF16)
        position_bias = sb("position_bias", [P, 3 * P])
        eps = sb("eps", [P, 1])
        zeros = sb("zeros", [P, D])
        pad_rows = sb("pad_rows", [P, REC])
        token_number = sb("token_number", [P, TILES_IN])
        region_start = sb("region_start", [P, EXPERTS])
        tile_number = sb("tile_number", [1, TILES])
        ones_row = sb("ones_row", [1, EXPERTS])

        ids_sb = sb("ids_sb", [P, TILES_IN], I32)
        wqk_sb = sb("wqk_sb", [P, D])
        wvt_sb = sb("wvt_sb", [P, D])
        bv_sb = sb("bv_sb", [P, D])
        router_w = sb("router_w", [P, SETS * PER_GROUP])
        router_b = sb("router_b", [P, SETS * PER_GROUP])
        w2_sb = sb("w2_sb", [P, EXPERTS * HID])

        gather_ids = sb("gather_ids", [P, 2, TC], I32)
        taps_of = sb("taps", [P, 2, TC, TAPS * D])
        h_of = within("h", late[0], [P, 2, TC, D])
        stats = sb("stats", [P, 2, TC, 6])
        half_sums = sb("half_sums", [P, 4, 2, TC])
        mean = sb("mean", [P, 2, TC])
        var = sb("var", [P, 2, TC])
        std = sb("std", [P, 2, TC])
        rstd = sb("rstd", [P, 2, TC])
        xn = within("xn", late[1], [P, TC, D])
        xT = within("xT", late[1] + TC * D, [P, 2, SEQ])
        qT = within("qT", late[1] + TC * D + 2 * SEQ, [P, 2, SEQ])
        v = within("v", late[1] + TC * D + 4 * SEQ, [P, 2, SEQ])
        attention_work = sb("attention_work", [P, 3, 2, 3 * P])
        scores, probs, pT = (attention_work[:, n, :, :] for n in range(3))
        neg_max = sb("neg_max", [P, 2, 2])
        row_sum = sb("row_sum", [P, 2, 2])
        row_inv = sb("row_inv", [P, 2, 2])
        h1_of = within("h1", late[0] + 2 * TC * D, [P, 2, TC, D])
        x2 = sb("x2", [P, TC, D])
        rows_of = sb("rows", [P, 2, TC, REC])
        x2T = within("x2T", 4 * WEIGHTS, [P, TC * P])

        NS = TC * SETS
        logits = sb("logits", [P, NS, PER_GROUP])
        set_max = sb("set_max", [P, NS])
        shifted = sb("shifted", [P, NS, PER_GROUP])
        choice = sb("choice", [P, NS, PER_GROUP])
        set_sum = sb("set_sum", [P, NS])
        set_inv = sb("set_inv", [P, NS])
        beats = sb("beats", [P, NS, 6])
        part = sb("part", [P, NS, PER_GROUP])
        rank = sb("rank", [P, NS, PER_GROUP])
        is_first = sb("is_first", [P, NS, PER_GROUP])
        is_second = sb("is_second", [P, NS, PER_GROUP])
        p_first = sb("p_first", [P, NS])
        p_second = sb("p_second", [P, NS])
        both = sb("both", [P, NS])
        kept_sum = sb("kept_sum", [P, NS])
        kept = sb("kept", [P, NS])
        kept_inv = sb("kept_inv", [P, NS])
        share = sb("share", [P, TC, SETS, PER_GROUP])
        group_share = sb("group_share", [P, TC, GROUPS])
        far = sb("far", [P, NS, PER_GROUP])
        group_slot = sb("group_slot", [P, TC, GROUPS])
        slot = sb("slot", [P, TC, GROUPS, PER_GROUP])
        chosen = sb("chosen", [P, TC, EXPERTS], BF16)
        next_row = sb("next_row", [P, EXPERTS])
        place = sb("place", [P, TC, EXPERTS])
        place_of = sb("place_of", [P, SLOTS, TC, EXPERTS])
        place_in = sb("place_in", [P, SLOTS, TC])
        send_to_of = sb("send_to", [P, 2, SLOTS, TC], I32)

        count = sb("count", [1, EXPERTS])
        count_i = sb("count_i", [1, EXPERTS], I32)
        tiles_i = sb("tiles_i", [1, EXPERTS], I32)
        tiles_of = sb("tiles_of", [1, EXPERTS])
        tiles_to = sb("tiles_to", [1, EXPERTS])
        passed = attention_work[0:1, :, :, :].rearrange("p a b n -> p (a b n)")[:, 0:TILES * EXPERTS].rearrange(
            "p (t e) -> p t e", e=EXPERTS)
        x2_space = x2[0:1, :, :].rearrange("p t n -> p (t n)")
        tile_expert, tile_in_region, tile_region = (x2_space[:, n * TILES:(n + 1) * TILES] for n in range(3))
        tiles_before = position_bias[0:1, 0:TILES]
        tile_row = sb("tile_row", [1, TILES], I32)
        tile_column = sb("tile_column", [1, TILES], I32)
        tile_weights = sb("tile_weights", [1, TILES], I32)
        pad_start = sb("pad_start", [1, EXPERTS], I32)

        xsT = within("xsT", 4 * WEIGHTS, [P, 2, 2, P], F32R)
        assert TC == 4 and RING <= TC and 5 * HID + RING * D <= 2 * TC * TAPS * D
        xs = rows_of[:, 0]
        taps_space = taps_of[:, :, :, :].rearrange("p a t n -> p (a t n)")
        gated = taps_space[:, 0:2 * HID].rearrange("p (r n) -> p r n", r=2)
        hid = taps_space[:, 2 * HID:4 * HID].rearrange("p (r n) -> p r n", r=2)
        hidT = taps_space[:, 4 * HID:5 * HID]
        y = taps_space[:, 5 * HID:5 * HID + RING * D].rearrange("p (r n) -> p r n", r=RING)
        add_to = sb("add_to", [P, RING], I32)

        ids_in = sem("ids_in")
        front_weights_in = sem("front_weights_in")
        weights_in = [sem(f"weights_in{n}") for n in range(2)]
        w2_in = sem("w2_in")
        high_ready = sem("high_ready")
        low_ready = sem("low_ready")
        pool_step = sem("pool_step")
        gather_ids_ready = sem("gather_ids_ready")
        shifts_ready = sem("shifts_ready")
        constants_ready = sem("constants_ready")
        gathered = [sem(f"gathered{n}") for n in range(2)]
        gather_begun = sem("gather_begun")
        send_begun = sem("send_begun")
        embedded = sem("embedded")
        h_ready = sem("h_ready")
        stats_ready = sem("stats_ready")
        var_ready = sem("var_ready")
        std_ready = sem("std_ready")
        xn_ready = sem("xn_ready")
        xn_transposed = sem("xn_transposed")
        xT_ready = sem("xT_ready")
        q_done = sem("q_done")
        v_done = sem("v_done")
        qT_ready = sem("qT_ready")
        v_ready = sem("v_ready")
        scores_done = sem("scores_done")
        max_ready = sem("max_ready")
        probs_ready = sem("probs_ready")
        probs_transposed = sem("probs_transposed")
        pT_ready = sem("pT_ready")
        pv_done = sem("pv_done")
        h1_ready = sem("h1_ready")
        h1_stored = [sem(f"h1_stored{n}") for n in range(2)]
        x2_ready = sem("x2_ready")
        x2_transposed = sem("x2_transposed")
        x2T_ready = sem("x2T_ready")
        logits_done = sem("logits_done")
        shifted_ready = sem("shifted_ready")
        choice_ready = sem("choice_ready")
        chosen_ready = sem("chosen_ready")
        places_done = sem("places_done")
        rows_copied = sem("rows_copied")
        rows_ready = sem("rows_ready")
        rows_sent = [sem(f"rows_sent{n}") for n in range(2)]
        vector_step = sem("vector_step")
        regions_ready = sem("regions_ready")
        table_ready = sem("table_ready")
        zeros_stored = sem("zeros_stored")
        pads_stored = sem("pads_stored")
        xs_in = [sem(f"xs_in{n}") for n in range(RING)]
        xs_transposed = sem("xs_transposed")
        xsT_high = sem("xsT_high")
        xsT_low = sem("xsT_low")
        gate_done = sem("gate_done")
        up_done = sem("up_done")
        gated_ready = sem("gated_ready")
        hid_ready = sem("hid_ready")
        low_transposed = sem("low_transposed")
        high_transposed = sem("high_transposed")
        hidT_low = sem("hidT_low")
        hidT_high = sem("hidT_high")
        down_done = sem("down_done")
        y_ready = sem("y_ready")
        y_free = sem("y_free")
        added = [sem(f"added{n}") for n in range(2)]
        sums_in = [sem(f"sums_in{n}") for n in range(LAST_CHUNKS)]
        out_ready = sem("out_ready")
        out_stored = sem("out_stored")


        sum_parts = [w[:, 0:TILES_IN * D].rearrange("p (c t n) -> p c t n", c=LAST_CHUNKS, n=D) for w in w_raw]

        def by_chunk(rows):
            return rows.rearrange("(c p t) n -> c p t n", p=P, c=LAST_CHUNKS)

        def older(c, b, n=BC):
            return c * n + max(b - 1, 0)

        block = ctx.enter_context(nc.Block())

        @block.sync
        def _(sp):
            sp.dma_start(ids_sb[:, :], ids).then_inc(ids_in, 16)
            for par in range(2):
                sp.sem_inc(h1_stored[par], 16)
            for dst, src in (
                (wqk_sb[:, :], w_qk), (wvt_sb[:, :], w_v_t), (bv_sb[:, :], b_v.partition_broadcast(P)),
                (router_w[:, 0:EXPERTS], w_gate), (router_w[:, EXPERTS:], w_route),
                (router_b[:, 0:EXPERTS], b_gate.partition_broadcast(P)),
                (router_b[:, EXPERTS:], b_route.partition_broadcast(P)),
            ):
                sp.dma_start(dst, src).then_inc(front_weights_in, 16)
            sp.wait_ge(constants_ready, 1)
            sp.wait_ge(gathered[1], 16 * TC)
            sp.wait_ge(gathered[0], 2 * 16 * TC)
            sp.dma_start(sums[1].rearrange("(t p) n -> p t n", p=P),
                         zeros[:, :].unsqueeze(1).broadcast_to([P, TILES_IN + 1, D])).then_inc(zeros_stored, 16)
            sp.dma_start(sums[0][TOKENS:, :], zeros[:, :]).then_inc(zeros_stored, 16)
            sp.dma_start(sent[EXPERTS * REGION:, :].rearrange("(t p) n -> p t n", p=P),
                         pad_rows[:, :].unsqueeze(1).broadcast_to([P, SPARE, REC])).then_inc(pads_stored, 16)
            with sp.Fori(0, CHUNKS // 2) as i:
                for par in range(2):
                    c = i * 2 + par
                    sp.wait_ge(h1_ready, c * BC + BC)
                    sp.dma_start(sums[0][bass.ds(c * (TC * P), TC * P), :].rearrange("(t p) n -> p t n", p=P),
                                 h1_of[:, par]).then_inc(h1_stored[par], 16)
                    at = bass.ds(c * PART, PART)
                    for dst, src, landed in ((w_raw[0], w1, weights_in[par]), (w_raw[1], w3, weights_in[par]),
                                             (w2_sb, w2, w2_in)):
                        sp.dma_start(dst[:, at], src[:, at]).then_inc(landed, 16)
            sp.wait_ge(regions_ready, 1)
            for e in range(EXPERTS):
                start = sp.value_load(pad_start[0:1, e:e + 1], min_val=0, max_val=EXPERTS * REGION - P)
                sp.dma_start(sent[bass.ds(start, P), :], pad_rows[:, :]).then_inc(pads_stored, 16)
            sp.wait_ge(table_ready, 1)
            sp.wait_ge(pads_stored, 16 * (EXPERTS + 1))
            for par in range(2):
                sp.wait_ge(rows_sent[par], 16 * CHUNKS // 2 * TC * SLOTS)

            def load(t, ring):
                row = sp.value_load(tile_row[0:1, bass.ds(t, 1)], min_val=0, max_val=SENT_ROWS - P)
                sp.dma_start(xs[:, ring, :], sent[bass.ds(row, P), :]).then_inc(xs_in[ring], 16)

            for n in range(RING):
                load(n, n)
            with sp.Fori(0, AHEAD // RING) as i:
                for n in range(RING):
                    sp.wait_ge(hid_ready, i * RING + n + 1)
                    load(i * RING + n + RING, n)
            sp.wait_ge(added[0], 16 * TILES // 2)
            sp.wait_ge(added[1], 16 * TILES // 2)
            for c in range(LAST_CHUNKS):
                for n in range(2):
                    sp.dma_start(sum_parts[n][:, c], by_chunk(sums[n][0:TOKENS, :])[c]).then_inc(sums_in[c], 16)
            sp.wait_ge(zeros_stored, 32)
            for par in range(2):
                sp.wait_ge(h1_stored[par], 16 * CHUNKS // 2 + 16)

        @block.gpsimd
        def _(pool):
            steps = [0]

            def step(ins):
                steps[0] += 1
                ins.then_inc(pool_step, 1)

            def settle():
                pool.wait_ge(pool_step, steps[0])

            def gather(par):
                for t in range(TC):
                    nc.gpsimd.indirect_dma_start(
                        out=taps_of[:, par, t, :], out_offset=None, in_=embedding[:, :],
                        in_offset=bass.IndirectOffsetOnAxis(ap=gather_ids[:, par, t:t + 1], axis=0)
                    ).then_inc(gathered[par], 16)

            def send(par):
                for s in range(SLOTS):
                    for t in range(TC):
                        nc.gpsimd.indirect_dma_start(
                            out=sent[:, :], out_offset=bass.IndirectOffsetOnAxis(ap=send_to_of[:, par, s, t:t + 1], axis=0),
                            in_=rows_of[:, par, t, :], in_offset=None).then_inc(rows_sent[par], 16)

            def next_gather(c, par, embedded_before):
                if embedded_before is not None:
                    pool.wait_ge(embedded, embedded_before)
                pool.tensor_copy(gather_ids[:, par, :], ids_sb[:, bass.ds(c * TC, TC)]).then_inc(gather_ids_ready, 1)
                pool.wait_ge(gather_ids_ready, c)
                pool.sem_inc(gather_begun, 1)
                gather(par)

            for m in (ident, from_before, from_after, last_to_first, first_to_last):
                step(nc.gpsimd.memset(m[:, :], 0.0))
            pool.wait_ge(ids_in, 16)
            step(nc.gpsimd.tensor_copy(gather_ids[:, 0, :], ids_sb[:, 0:TC]))
            settle()
            gather(0)
            for m, base, per_partition in ((ident, 0, -1), (from_before, -1, -1), (from_after, 1, -1),
                                           (last_to_first, P * (P - 1), -P), (first_to_last, -(P - 1), P)):
                step(nc.gpsimd.affine_select(out=m[:, :], in_=m[:, :], pattern=[[1, P]],
                                             compare_op=ALU.not_equal, fill=1.0, base=base,
                                             channel_multiplier=per_partition))
            settle()
            pool.sem_inc(shifts_ready, 1)
            next_gather(1, 1, None)
            step(nc.gpsimd.memset(ones[:, :], 1.0))
            settle()
            step(nc.gpsimd.affine_select(out=earlier[:, :], in_=ones[:, :], pattern=[[1, P]],
                                         compare_op=ALU.is_gt, fill=0.0, base=0, channel_multiplier=-1))
            step(nc.gpsimd.iota(position_bias[:, 0:P], pattern=[[1, P]], base=0, channel_multiplier=-1,
                                allow_small_or_imprecise_dtypes=True))
            step(nc.gpsimd.iota(position_bias[:, P:], pattern=[[1, 2 * P]], base=-P, channel_multiplier=-1,
                                allow_small_or_imprecise_dtypes=True))
            settle()
            step(nc.gpsimd.tensor_scalar(position_bias[:, :], position_bias[:, :], SLOPE, None, ALU.mult))
            settle()
            for cols, base in ((position_bias[:, 0:P], 0), (position_bias[:, P:], P)):
                step(nc.gpsimd.affine_select(out=cols, in_=cols, pattern=[[-1, cols.shape[1]]],
                                             compare_op=ALU.is_ge, fill=MASKED, base=base, channel_multiplier=1))
            step(nc.gpsimd.memset(eps[:, :], EPS))
            step(nc.gpsimd.memset(zeros[:, :], 0.0))
            step(nc.gpsimd.memset(pad_rows[:, 0:REC - 1], 0.0))
            step(nc.gpsimd.iota(pad_rows[:, REC - 1:], pattern=[[0, 1]], base=TOKENS, channel_multiplier=1,
                                allow_small_or_imprecise_dtypes=True))
            step(nc.gpsimd.iota(token_number[:, :], pattern=[[P, TILES_IN]], base=0, channel_multiplier=1,
                                allow_small_or_imprecise_dtypes=True))
            for m in (region_start, next_row):
                step(nc.gpsimd.iota(m[:, :], pattern=[[REGION, EXPERTS]], base=0, channel_multiplier=0,
                                    allow_small_or_imprecise_dtypes=True))
            step(nc.gpsimd.iota(tile_number[:, :], pattern=[[1, TILES]], base=0, channel_multiplier=0,
                                allow_small_or_imprecise_dtypes=True))
            step(nc.gpsimd.memset(ones_row[:, :], 1.0))
            settle()
            pool.sem_inc(constants_ready, 1)

            def next_send(c, par):
                pool.wait_ge(rows_ready, c + 2)
                pool.sem_inc(send_begun, 1)
                send(par)

            next_gather(2, 0, BC)
            with pool.Fori(0, (CHUNKS - 3) // 2) as i:
                for par in range(2):
                    next_gather(i * 2 + (par + 3), 1 - par, i * (2 * BC) + (par + 2) * BC)
                    next_send(i * 2 + par, par)
            for c in range((CHUNKS - 3) // 2 * 2, CHUNKS):
                if c + 3 < CHUNKS:
                    next_gather(c + 3, (c + 3) % 2, (c + 2) * BC)
                next_send(c, c % 2)

            pool.sem_inc(y_free, 2)
            pool.wait_ge(zeros_stored, 32)
            for par in range(2):
                pool.wait_ge(h1_stored[par], 16 * CHUNKS // 2 + 16)

            def add(t, n, added_before):
                pool.wait_ge(y_ready, t + 2)
                if added_before is not None:
                    pool.wait_ge(added[n % 2], added_before)
                pool.sem_inc(y_free, 1)
                nc.gpsimd.indirect_dma_start(
                    out=sums[n % 2][:, :], out_offset=bass.IndirectOffsetOnAxis(ap=add_to[:, n:n + 1], axis=0),
                    in_=y[:, n, :], in_offset=None, compute_op=ALU.add).then_inc(added[n % 2], 16)

            for n in range(2):
                add(n, n, None)
            with pool.Fori(0, TILES // RING - 1) as i:
                for n in range(RING):
                    add(i * RING + (n + 2), (n + 2) % RING, i * (16 * RING // 2) + 16 * (n // 2 + 1))
            for n in range(2):
                add(TILES - 2 + n, RING - 2 + n, 16 * (TILES // 2 - 1))

        @block.scalar
        def _(act):

            def copy_xT(c, b):
                act.wait_ge(xn_transposed, c * BC + b + 1)
                act.wait_ge(scores_done, older(c, b))
                nc.scalar.copy(xT[:, b % 2, :], bank[2][:, 0:SEQ]).then_inc(xT_ready, 1)

            def copy_qT(c, b):
                act.wait_ge(q_done, c * BC + b + 1)
                nc.scalar.copy(qT[:, b % 2, :], bank[3][:, 0:SEQ]).then_inc(qT_ready, 1)

            def exponentials(c, b):
                act.wait_ge(max_ready, c * BC + b + 1)
                act.wait_ge(probs_transposed, older(c, b))
                act.wait_ge(h1_ready, older(c, b))
                nc.scalar.activation(probs[:, b % 2, 0:P], scores[:, b % 2, 0:P], ACT.Exp,
                                     bias=neg_max[:, b % 2, 0:1], accum_out=row_sum[:, b % 2, 0:1])
                nc.scalar.activation(probs[:, b % 2, P:], scores[:, b % 2, P:], ACT.Exp,
                                     bias=neg_max[:, b % 2, 1:2], accum_out=row_sum[:, b % 2, 1:2]
                                     ).then_inc(probs_ready, 1)

            def copy_pT(c, b):
                act.wait_ge(probs_transposed, c * BC + b + 1)
                act.wait_ge(pv_done, older(c, b))
                nc.scalar.copy(pT[:, b % 2, :], bank[6][:, 0:3 * P]).then_inc(pT_ready, 1)

            def split(c, par, loads, piece):
                if piece == 0:
                    act.wait_ge(weights_in[par], loads)
                n, at = piece % 2, bass.ds(c * PART + piece // 2 * HID, HID)
                nc.scalar.copy(w_high[n][:, at], w_raw[n][:, at]).then_inc(high_ready, 1)

            def embedding(c, par, b):
                act.wait_ge(embedded, c * BC + b + 1)
                nc.scalar.copy(h_of[:, par, 2 * b:2 * b + 2, :].rearrange("p t n -> p (t n)"),
                               bank[b][:, 0:SEQ]).then_inc(h_ready, 1)

            def roots(which, count):
                act.wait_ge(var_ready, count)
                nc.scalar.activation(std[:, which, :], var[:, which, :], ACT.Sqrt, bias=eps[:, 0:1],
                                     scale=0.25).then_inc(std_ready, 1)

            def copies(c, b):
                copy_xT(c, b)
                copy_qT(c, b)

            def attend_and_choose(k, par, loads, a_too, b_too):
                if loads is not None:
                    for piece in range(PIECES // 2):
                        split(k, par, loads, piece)
                if b_too:
                    exponentials(k + 1, 0)
                if a_too:
                    act.wait_ge(h1_ready, k * BC + BC)
                    embedding(k + 2, par, 0)
                act.wait_ge(shifted_ready, k + 1)
                nc.scalar.activation(choice[:, :, :], shifted[:, :, :], ACT.Exp).then_inc(choice_ready, 1)
                if b_too:
                    copy_pT(k + 1, 0)
                    exponentials(k + 1, 1)
                    if a_too:
                        embedding(k + 2, par, 1)
                    copy_pT(k + 1, 1)
                if loads is not None:
                    for piece in range(PIECES // 2, PIECES):
                        split(k, par, loads, piece)

            def prepare(k, par, sent_before, a_too):
                roots(slice(0, 2) if a_too else slice(1, 2), k + 3)
                if a_too:
                    copies(k + 2, 0)
                act.wait_ge(x2_transposed, k + 2)
                act.wait_ge(logits_done, k + 1)
                nc.scalar.copy(x2T[:, :], bank[0][:, :]).then_inc(x2T_ready, 1)
                if a_too:
                    copies(k + 2, 1)
                if sent_before is not None:
                    act.wait_ge(rows_sent[1 - par], sent_before)
                nc.scalar.copy(rows_of[:, 1 - par, :, 0:D], x2[:, :, :]).then_inc(rows_copied, 1)

            for b in range(BC):
                embedding(0, 0, b)
            act.wait_ge(constants_ready, 1)
            roots(slice(0, 1), 1)
            for b in range(BC):
                embedding(1, 1, b)
            for b in range(BC):
                copies(0, b)
            for b in range(BC):
                exponentials(0, b)
                copy_pT(0, b)
            prepare(-1, 1, None, True)
            per_half = 16 * TC * SLOTS
            attend_and_choose(0, 0, 32, True, True)
            prepare(0, 0, None, True)
            with act.Fori(0, FRONT - 1) as i:
                for n in range(2):
                    k, par = i * 2 + (n + 1), 1 - n
                    attend_and_choose(k, par, i * 32 + 32 * (n + 1), True, True)
                    prepare(k, par, i * per_half + per_half, True)
            attend_and_choose(CHUNKS - 3, 1, 32 * FRONT, True, True)
            prepare(CHUNKS - 3, 1, FRONT * per_half, True)
            attend_and_choose(CHUNKS - 2, 0, None, False, True)
            prepare(CHUNKS - 2, 0, FRONT * per_half, False)
            attend_and_choose(CHUNKS - 1, 1, None, False, False)
            act.wait_ge(x2_ready, CHUNKS)
            for par in range(2):
                act.wait_ge(h1_stored[par], 16 * CHUNKS // 2 + 16)
            act.wait_ge(scores_done, CHUNKS * BC)
            act.wait_ge(pv_done, CHUNKS * BC)
            for c in (CHUNKS - 2, CHUNKS - 1):
                for piece in range(PIECES):
                    split(c, c % 2, 16 * CHUNKS, piece)

            def copy_xsT(t, ring):
                act.wait_ge(xs_transposed, t + 1)
                nc.scalar.copy(xsT[:, ring % 2, 0, :], bank[6][:, 0:P]).then_inc(xsT_high, 1)

            def silu(t, ring):
                act.wait_ge(gate_done, t + 1)
                nc.scalar.activation(gated[:, ring % 2, :], bank[ring % 2][:, :], ACT.Silu).then_inc(gated_ready, 1)

            def step(j, n, rest):
                if rest > 1:
                    silu(j + 1, n + 1)
                act.wait_ge(low_transposed, j + 1)
                nc.scalar.copy(hidT[:, 0:HID // 2], bank[4][:, 0:HID // 2]).then_inc(hidT_low, 1)
                if rest > 2:
                    copy_xsT(j + 2, n + 2)

            copy_xsT(0, 0)
            copy_xsT(1, 1)
            silu(0, 0)
            with act.Fori(0, AHEAD // RING) as i:
                for n in range(RING):
                    step(i * RING + n, n, RING)
            for n in range(RING):
                step(AHEAD + n, n, RING - n)

            for c in range(LAST_CHUNKS):
                act.wait_ge(out_ready, c + 1)
                act.dma_start(by_chunk(out.rearrange("b s n -> (b s) n"))[c], sum_parts[0][:, c]).then_inc(out_stored, 16)
            act.wait_ge(out_stored, 16 * LAST_CHUNKS)

        @block.vector
        def _(dve):
            steps = [0]
            before = [0]

            def link(ins):
                steps[0] += 1
                ins.then_inc(vector_step, 1)
                dve.wait_ge(vector_step, before[0] + steps[0])

            def cells(ap, shape):
                return ap.broadcast_to(shape)

            tt, ts, stt = nc.vector.tensor_tensor, nc.vector.tensor_scalar, nc.vector.scalar_tensor_tensor

            def values_and_scores(c, b):
                dve.wait_ge(v_done, c * BC + b + 1)
                dve.wait_ge(pv_done, older(c, b))
                tt(v[:, b % 2, :].rearrange("p (t n) -> p t n", t=2),
                   bank[5][:, 0:SEQ].rearrange("p (t n) -> p t n", t=2),
                   cells(bv_sb[:, :].unsqueeze(1), [P, 2, D]), ALU.add).then_inc(v_ready, 1)
                dve.wait_ge(scores_done, c * BC + b + 1)
                dve.wait_ge(probs_ready, older(c, b))
                link(stt(scores[:, b % 2, :], bank[4][:, 0:3 * P], SCALE, position_bias[:, :],
                         ALU.mult, ALU.add))
                nc.vector.tensor_reduce(neg_max[:, b % 2, 0:1], scores[:, b % 2, 0:P], AX.X, ALU.max, negate=True)
                nc.vector.tensor_reduce(neg_max[:, b % 2, 1:2], scores[:, b % 2, P:], AX.X, ALU.max,
                                        negate=True).then_inc(max_ready, 1)

            def residual(c, par, b, stored):
                h, h1 = h_of[:, par], h1_of[:, par]
                if b == 0 and stored is not None:
                    dve.wait_ge(h1_stored[par], stored + 16)
                dve.wait_ge(probs_ready, c * BC + b + 1)
                link(nc.vector.reciprocal(row_inv[:, b % 2, :], row_sum[:, b % 2, :]))
                dve.wait_ge(pv_done, c * BC + b + 1)
                for t in range(2):
                    last = stt(h1[:, 2 * b + t, :], bank[7][:, t * D:(t + 1) * D], row_inv[:, b % 2, t:t + 1],
                               h[:, 2 * b + t, :], ALU.mult, ALU.add)
                link(last)
                for t in range(2):
                    last = nc.vector.bn_stats(stats[:, 1, 2 * b + t, :], h1[:, 2 * b + t, :])
                last.then_inc(h1_ready, 1)

            def moments(which):
                summed, apart, squares, square = (half_sums[:, n, which, :] for n in range(4))
                of = stats[:, which]
                tt(summed, of[:, :, :, 1], of[:, :, :, 4], ALU.add)
                tt(apart, of[:, :, :, 1], of[:, :, :, 4], ALU.subtract)
                link(tt(squares, of[:, :, :, 2], of[:, :, :, 5], ALU.add))
                ts(mean[:, which, :], summed, 0.5, None, ALU.mult)
                link(tt(square, apart, apart, ALU.mult))
                stt(var[:, which, :], squares, 4.0 / D, square, ALU.mult, ALU.add).then_inc(var_ready, 1)

            all4 = [P, NS, PER_GROUP]

            def shifted_logits(c):
                dve.wait_ge(logits_done, c + 1)
                link(tt(logits[:, :, :].rearrange("p (t g) e -> p t (g e)", g=SETS),
                        bank[3][:, 0:TC * SETS * PER_GROUP].rearrange("p (t n) -> p t n", t=TC),
                        cells(router_b[:, :].unsqueeze(1), [P, TC, SETS * PER_GROUP]), ALU.add))
                link(nc.vector.tensor_reduce(set_max[:, :], logits[:, :, :], AX.X, ALU.max))
                tt(shifted[:, :, :], logits[:, :, :], cells(set_max[:, :].unsqueeze(2), all4),
                   ALU.subtract).then_inc(shifted_ready, 1)

            def softmaxes(c):
                dve.wait_ge(choice_ready, c + 1)
                link(nc.vector.tensor_reduce(set_sum[:, :], choice[:, :, :], AX.X, ALU.add))
                link(nc.vector.reciprocal(set_inv[:, :], set_sum[:, :]))
                link(tt(choice[:, :, :], choice[:, :, :], cells(set_inv[:, :].unsqueeze(2), all4), ALU.mult))

            def pair(n):
                return beats[:, :, n:n + 1]

            slots = slot[:, :, :, :].rearrange("p t g e -> p t (g e)")

            def choose():
                for i, at in ((0, 0), (1, 3), (2, 5)):
                    n = PER_GROUP - 1 - i
                    last = tt(beats[:, :, at:at + n], cells(choice[:, :, i:i + 1], [P, NS, n]),
                              choice[:, :, i + 1:], ALU.is_ge)
                link(last)
                tt(part[:, :, 0:1], pair(0), pair(1), ALU.add)
                tt(part[:, :, 1:2], pair(3), pair(4), ALU.add)
                tt(part[:, :, 2:3], pair(1), pair(3), ALU.add)
                link(tt(part[:, :, 3:4], pair(2), pair(4), ALU.add))
                tt(rank[:, :, 0:1], part[:, :, 0:1], pair(2), ALU.add)
                stt(rank[:, :, 1:2], pair(0), 2.0, part[:, :, 1:2], ALU.add, ALU.subtract)
                stt(rank[:, :, 2:3], part[:, :, 2:3], 1.0, pair(5), ALU.add, ALU.subtract)
                link(tt(rank[:, :, 3:4], part[:, :, 3:4], pair(5), ALU.add))
                link(ts(rank[:, :, 0:1], rank[:, :, 0:1], -1.0, 3.0, ALU.mult, ALU.add))
                ts(far[:, :, :], rank[:, :, :], 2.0, 8.0, ALU.is_ge, ALU.mult)
                ts(is_first[:, :, :], rank[:, :, :], 0.0, None, ALU.is_equal)
                link(ts(is_second[:, :, :], rank[:, :, :], 1.0, None, ALU.is_equal))
                far_of = far[:, :, :].rearrange("p (t g) e -> p t g e", g=SETS)
                rank_of = rank[:, :, :].rearrange("p (t g) e -> p t g e", g=SETS)
                stt(group_slot[:, :, :], rank_of[:, :, GROUPS, :], 2.0, far_of[:, :, GROUPS, :], ALU.mult, ALU.add)
                link(tt(slot[:, :, :, :], rank_of[:, :, 0:GROUPS, :], far_of[:, :, 0:GROUPS, :], ALU.add))
                link(tt(slot[:, :, :, :], slot[:, :, :, :],
                        cells(group_slot[:, :, :].unsqueeze(3), [P, TC, GROUPS, PER_GROUP]), ALU.add))
                ts(chosen[:, :, :], slots, float(SLOTS), None, ALU.is_lt).then_inc(chosen_ready, 1)

            def weigh_first():
                tt(part[:, :, :], choice[:, :, :], is_first[:, :, :], ALU.mult)
                link(tt(shifted[:, :, :], choice[:, :, :], is_second[:, :, :], ALU.mult))
                nc.vector.tensor_reduce(p_first[:, :], part[:, :, :], AX.X, ALU.add)
                link(nc.vector.tensor_reduce(p_second[:, :], shifted[:, :, :], AX.X, ALU.add))
                link(tt(both[:, :], p_first[:, :], p_second[:, :], ALU.add))
                link(stt(kept[:, :], both[:, :], KEEP, p_second[:, :], ALU.is_le, ALU.mult))

            def weigh_last(c, par):
                tt(shifted[:, :, :], is_second[:, :, :], cells(kept[:, :].unsqueeze(2), all4), ALU.mult)
                link(stt(kept_sum[:, :], kept[:, :], 1e-9, p_first[:, :], ALU.add, ALU.add))
                tt(part[:, :, :], part[:, :, :], shifted[:, :, :], ALU.add)
                link(nc.vector.reciprocal(kept_inv[:, :], kept_sum[:, :]))
                shares = share[:, :, :, :].rearrange("p t g e -> p (t g) e")
                link(tt(shares, part[:, :, :], cells(kept_inv[:, :].unsqueeze(2), all4), ALU.mult))
                link(ts(group_share[:, :, :], share[:, :, GROUPS, :], float(GROUPS) ** -0.5, None, ALU.mult))
                dve.wait_ge(rows_copied, c + 1)
                tt(rows_of[:, par, :, D:D + EXPERTS].rearrange("p t (g e) -> p t g e", g=GROUPS),
                   share[:, :, 0:GROUPS, :],
                   cells(group_share[:, :, :].unsqueeze(3), [P, TC, GROUPS, PER_GROUP]), ALU.mult)
                nc.vector.tensor_copy(rows_of[:, par, :, REC - 1], token_number[:, bass.ds(c * TC, TC)])

            def locate(c, par):
                dve.wait_ge(places_done, c + 1)
                link(tt(place[:, :, :], bank[6][:, 0:TC * EXPERTS].rearrange("p (t e) -> p t e", t=TC),
                        cells(next_row[:, :].unsqueeze(1), [P, TC, EXPERTS]), ALU.add))
                tt(next_row[:, :], next_row[:, :], bank[6][:, TC * EXPERTS:(TC + 1) * EXPERTS], ALU.add)
                for s in range(SLOTS):
                    last = stt(place_of[:, s], slots, float(s), place[:, :, :], ALU.is_equal, ALU.mult)
                link(last)
                link(nc.vector.tensor_reduce(place_in[:, :, :], place_of[:, :, :, :], AX.X, ALU.add))
                nc.vector.tensor_copy(send_to_of[:, par], place_in[:, :, :]).then_inc(rows_ready, 1)

            def split(c, number, piece):
                n, at = piece % 2, bass.ds(c * PART + piece // 2 * HID, HID)
                dve.wait_ge(high_ready, number * PIECES + (piece + 1))
                tt(w_low[n][:, at], w_raw[n][:, at], w_high[n][:, at].bitcast(F32),
                   ALU.subtract).then_inc(low_ready, 1)

            def embedding_stats(c, par):
                for b in range(BC):
                    dve.wait_ge(h_ready, c * BC + b + 1)
                    for t in (2 * b, 2 * b + 1):
                        last = nc.vector.bn_stats(stats[:, 0, t, :], h_of[:, par, t, :])
                return last

            def normalised(out, which, of, t):
                return ts(out[:, t, :], of[:, t, :], mean[:, which, t:t + 1], rstd[:, which, t:t + 1],
                          ALU.subtract, ALU.mult)

            def normalise(c, par):
                dve.wait_ge(xn_transposed, c * BC)
                for t in range(TC):
                    last = normalised(xn, 0, h_of[:, par], t)
                    if t % 2:
                        last.then_inc(xn_ready, 1)

            def normalise_again(c, par):
                dve.wait_ge(x2_transposed, c)
                dve.wait_ge(rows_copied, c)
                for t in range(TC):
                    last = normalised(x2, 1, h1_of[:, par], t)
                last.then_inc(x2_ready, 1)

            def attend_and_choose(k, par, stored, a_too, b_too):
                shifted_logits(k)
                softmaxes(k)
                if a_too:
                    split(k, k, 0)
                if b_too:
                    residual(k + 1, 1 - par, 0, stored)
                choose()
                if a_too:
                    embedding_stats(k + 2, par)
                if b_too:
                    residual(k + 1, 1 - par, 1, None)

            def prepare(k, par, a_too, routed):
                dve.wait_ge(h1_ready, k * BC + 2 * BC)
                moments(slice(0, 2) if a_too else slice(1, 2))
                if routed:
                    weigh_first()
                dve.wait_ge(std_ready, k + 3)
                which = slice(0, 2) if a_too else slice(1, 2)
                link(nc.vector.reciprocal(rstd[:, which, :], std[:, which, :]))
                if a_too:
                    normalise(k + 2, par)
                normalise_again(k + 1, 1 - par)
                if routed:
                    weigh_last(k, par)
                if a_too:
                    if routed:
                        for piece in range(1, PIECES - 1):
                            split(k, k, piece)
                    values_and_scores(k + 2, 0)
                if routed:
                    locate(k, par)
                if a_too:
                    values_and_scores(k + 2, 1)
                    if routed:
                        split(k, k, PIECES - 1)

            dve.sem_inc(rows_ready, 1)
            dve.sem_inc(y_ready, 1)
            link(embedding_stats(0, 0))
            moments(slice(0, 1))
            dve.wait_ge(std_ready, 1)
            link(nc.vector.reciprocal(rstd[:, 0, :], std[:, 0, :]))
            normalise(0, 0)
            dve.wait_ge(constants_ready, 1)
            dve.wait_ge(front_weights_in, 16 * 7)
            for b in range(BC):
                values_and_scores(0, b)
            embedding_stats(1, 1)
            for b in range(BC):
                residual(0, 0, b, None)
            prepare(-1, 1, True, False)
            counted = steps[0]
            with dve.Fori(0, FRONT) as i:
                before[0], steps[0] = i * VECTOR_PER_PASS + counted, 0
                for par in range(2):
                    attend_and_choose(i * 2 + par, par, (i + par) * 16, True, True)
                    prepare(i * 2 + par, par, True, True)
            assert steps[0] == VECTOR_PER_PASS, steps[0]
            before[0], steps[0] = counted + FRONT * VECTOR_PER_PASS, 0
            attend_and_choose(CHUNKS - 2, 0, FRONT * 16, False, True)
            prepare(CHUNKS - 2, 0, False, True)
            attend_and_choose(CHUNKS - 1, 1, None, False, False)
            weigh_first()
            weigh_last(CHUNKS - 1, 1)
            locate(CHUNKS - 1, 1)

            by_tile = [1, TILES, EXPERTS]
            nc.vector.tensor_copy(pad_start[:, :], next_row[0:1, :]).then_inc(regions_ready, 1)
            link(tt(count[:, :], next_row[0:1, :], region_start[0:1, :], ALU.subtract))
            link(ts(count_i[:, :], count[:, :], float(P - 1), None, ALU.add))
            link(ts(tiles_i[:, :], count_i[:, :], P.bit_length() - 1, None, ALU.logical_shift_right))
            link(nc.vector.tensor_copy(tiles_of[:, :], tiles_i[:, :]))
            link(nc.vector.tensor_tensor_scan(tiles_to[:, :], ones_row[:, :], tiles_of[:, :], 0.0,
                                              ALU.mult, ALU.add))
            link(tt(passed[:, :, :], cells(tiles_to[:, :].unsqueeze(1), by_tile),
                    cells(tile_number[:, :].unsqueeze(2), by_tile), ALU.is_le))
            link(nc.vector.tensor_reduce(tile_expert[:, :], passed[:, :, :], AX.X, ALU.add))
            link(tt(passed[:, :, :], passed[:, :, :], cells(tiles_of[:, :].unsqueeze(1), by_tile), ALU.mult))
            link(nc.vector.tensor_reduce(tiles_before[:, :], passed[:, :, :], AX.X, ALU.add))
            tt(tile_in_region[:, :], tile_number[:, :], tiles_before[:, :], ALU.subtract)
            link(ts(tile_region[:, :], tile_expert[:, :], float(REGION), None, ALU.mult))
            stt(tile_row[:, :], tile_in_region[:, :], float(P), tile_region[:, :], ALU.mult, ALU.add)
            ts(tile_column[:, :], tile_expert[:, :], float(EXPERTS - 1), float(D), ALU.min, ALU.add)
            ts(tile_weights[:, :], tile_expert[:, :], float(EXPERTS - 1), float(HID), ALU.min,
               ALU.mult).then_inc(table_ready, 1)
            for c in (CHUNKS - 2, CHUNKS - 1):
                for piece in range(PIECES):
                    split(c, c, piece)

            def low_of_xs(t, n):
                dve.wait_ge(xsT_high, t + 1)
                tt(xsT[:, n % 2, 1, :], bank[6][:, 0:P], xsT[:, n % 2, 0, :].bitcast(F32),
                   ALU.subtract).then_inc(xsT_low, 1)

            def column_of(t):
                return dve.value_load(tile_column[0:1, bass.ds(t, 1)], min_val=D, max_val=D + EXPERTS - 1)

            def hidden_begin(t, n):
                dve.wait_ge(xs_in[n % RING], (t + 1 - (n % RING)) * (16 // RING) + (16 - 16 // RING))
                dve.wait_ge(y_free, t + 1)
                nc.vector.tensor_copy(add_to[:, n % RING:n % RING + 1], xs[:, n % RING, REC - 1:])

            def hidden(t, n, column):
                dve.wait_ge(up_done, t + 1)
                dve.wait_ge(gated_ready, t + 1)
                stt(hid[:, n % 2, :], gated[:, n % 2, :], xs[:, n % RING, bass.ds(column, 1)], bank[2 + n % 2][:, :],
                    ALU.mult, ALU.mult).then_inc(hid_ready, 1)

            def step(j, n, rest):
                if rest > 1:
                    column = column_of(j + 1)
                dve.wait_ge(high_transposed, j + 1)
                nc.vector.tensor_copy(hidT[:, HID // 2:], bank[5][:, 0:HID // 2]).then_inc(hidT_high, 1)
                if rest > 1:
                    hidden_begin(j + 1, n + 1)
                if rest > 2:
                    low_of_xs(j + 2, n + 2)
                if rest > 1:
                    hidden(j + 1, n + 1, column)
                dve.wait_ge(down_done, j + 1)
                nc.vector.tensor_copy(y[:, n, :], bank[7][:, 0:D]).then_inc(y_ready, 1)

            dve.wait_ge(table_ready, 1)
            low_of_xs(0, 0)
            low_of_xs(1, 1)
            hidden_begin(0, 0)
            hidden(0, 0, column_of(0))
            with dve.Fori(0, AHEAD // RING) as i:
                for n in range(RING):
                    step(i * RING + n, n, RING)
            for n in range(RING):
                step(AHEAD + n, n, RING - n)

            for c in range(LAST_CHUNKS):
                dve.wait_ge(sums_in[c], 32)
                first, second = (part[:, c] for part in sum_parts)
                tt(first, first, second, ALU.add).then_inc(out_ready, 1)

        @block.tensor
        def _(pe):
            mm = nc.tensor.matmul
            pe.wait_ge(shifts_ready, 1)

            def embed(taps, b):
                to = bank[b]
                whole = to[:, 0:SEQ].rearrange("p (t n) -> p t n", t=2)
                first, second = to[:, 0:D], to[:, D:SEQ]
                pair = taps[:, 2 * b:2 * b + 2, :]
                mm(whole, from_before[:, :], pair[:, :, 0:D], start=True, stop=False)
                mm(second, last_to_first[:, :], taps[:, 2 * b, 0:D], start=False, stop=False)
                mm(whole, ident[:, :], pair[:, :, D:2 * D], start=False, stop=False)
                mm(whole, from_after[:, :], pair[:, :, 2 * D:3 * D], start=False, stop=False)
                mm(first, first_to_last[:, :], taps[:, 2 * b + 1, 2 * D:3 * D],
                   start=False, stop=True).then_inc(embedded, 1)

            def to_scores(c, b, logits_before=None):
                pe.wait_ge(xn_ready, c * BC + b + 1)
                pe.wait_ge(xT_ready, c * BC + b)
                for t in range(2):
                    last = nc.tensor.transpose(bank[2][:, t * P:(t + 1) * P], xn[:, 2 * b + t, :], ident[:, :])
                last.then_inc(xn_transposed, 1)
                pe.wait_ge(xT_ready, c * BC + b + 1)
                pe.wait_ge(qT_ready, c * BC + b)
                if b == 0 and logits_before is not None:
                    pe.wait_ge(shifted_ready, logits_before)
                mm(bank[3][:, 0:SEQ], wqk_sb[:, :], xT[:, b % 2, :], start=True, stop=True).then_inc(q_done, 1)
                pe.wait_ge(v_ready, c * BC + b)
                for t in range(2):
                    last = mm(bank[5][:, t * D:(t + 1) * D], xT[:, b % 2, t * P:(t + 1) * P],
                              wvt_sb[:, :], start=True, stop=True)
                last.then_inc(v_done, 1)
                pe.wait_ge(qT_ready, c * BC + b + 1)
                pe.wait_ge(max_ready, c * BC + b)
                mm(bank[4][:, 0:P], qT[:, b % 2, 0:P], xT[:, b % 2, 0:P], start=True, stop=True)
                mm(bank[4][:, P:3 * P], qT[:, b % 2, P:], xT[:, b % 2, :],
                   start=True, stop=True).then_inc(scores_done, 1)

            def attend(c, b, places_before=None):
                pe.wait_ge(probs_ready, c * BC + b + 1)
                pe.wait_ge(pT_ready, c * BC + b)
                if b == 0 and places_before is not None:
                    pe.wait_ge(rows_ready, places_before + 1)
                for n in range(3):
                    last = nc.tensor.transpose(bank[6][:, n * P:(n + 1) * P], probs[:, b % 2, n * P:(n + 1) * P],
                                               ident[:, :])
                last.then_inc(probs_transposed, 1)
                pe.wait_ge(pT_ready, c * BC + b + 1)
                pe.wait_ge(v_ready, c * BC + b + 1)
                pe.wait_ge(h1_ready, c * BC + b)
                mm(bank[7][:, 0:D], pT[:, b % 2, 0:P], v[:, b % 2, 0:D], start=True, stop=True)
                mm(bank[7][:, D:SEQ], pT[:, b % 2, P:2 * P], v[:, b % 2, 0:D], start=True, stop=False)
                mm(bank[7][:, D:SEQ], pT[:, b % 2, 2 * P:], v[:, b % 2, D:],
                   start=False, stop=True).then_inc(pv_done, 1)

            def transpose_x2(k, embedded_before):
                pe.wait_ge(x2_ready, k + 1)
                pe.wait_ge(h_ready, embedded_before)
                for t in range(TC):
                    last = nc.tensor.transpose(bank[0][:, t * P:(t + 1) * P], x2[:, t, :], ident[:, :])
                last.then_inc(x2_transposed, 1)

            def route(k, queries_before):
                pe.wait_ge(qT_ready, queries_before)
                pe.wait_ge(x2T_ready, k + 1)
                wide = SETS * PER_GROUP
                for t in range(TC):
                    last = mm(bank[3][:, t * wide:(t + 1) * wide], x2T[:, t * P:(t + 1) * P], router_w[:, :],
                              start=True, stop=True)
                last.then_inc(logits_done, 1)

            def count_places(k, probs_before):
                pe.wait_ge(chosen_ready, k + 1)
                pe.wait_ge(pT_ready, probs_before)
                n = TC * EXPERTS
                mm(bank[6][:, 0:n], earlier[:, :], chosen[:, :, :].rearrange("p t e -> p (t e)"),
                   start=True, stop=False)
                for t in range(TC - 1):
                    mm(bank[6][:, (t + 1) * EXPERTS:n].rearrange("p (t e) -> p t e", e=EXPERTS), ones[:, :],
                       chosen[:, t:t + 1, :].broadcast_to([P, TC - 1 - t, EXPERTS]),
                       start=False, stop=(t == TC - 2))
                for t in range(TC):
                    last = mm(bank[6][:, n:n + EXPERTS], ones[:, :], chosen[:, t, :], start=(t == 0),
                              stop=(t == TC - 1))
                last.then_inc(places_done, 1)

            def embed_first(par, through):
                pe.wait_ge(gathered[par], through)
                embed(taps_of[:, par], 0)

            def attend_and_choose(k, par, gathered_through, b_too):
                if gathered_through is not None:
                    embed_first(par, gathered_through)
                if b_too:
                    attend(k + 1, 0, k)
                if gathered_through is not None:
                    embed(taps_of[:, par], 1)
                if b_too:
                    attend(k + 1, 1)

            def prepare(k, a_too, routed, through):
                if routed:
                    count_places(k, k * BC + 2 * BC)
                if a_too:
                    to_scores(k + 2, 0, k + 1)
                transpose_x2(k + 1, through)
                if a_too:
                    to_scores(k + 2, 1)
                route(k + 1, through)

            embed_first(0, 16 * TC)
            embed(taps_of[:, 0], 1)
            pe.wait_ge(h_ready, BC)
            embed_first(1, 16 * TC)
            embed(taps_of[:, 1], 1)
            pe.wait_ge(front_weights_in, 16 * 7)
            pe.wait_ge(constants_ready, 1)
            for b in range(BC):
                to_scores(0, b)
            for b in range(BC):
                attend(0, b)
            prepare(-1, True, False, 2 * BC)
            with pe.Fori(0, FRONT) as i:
                for par in range(2):
                    k = i * 2 + par
                    attend_and_choose(k, par, i * (16 * TC) + 2 * (16 * TC), True)
                    prepare(k, True, True, k * BC + 3 * BC)
            attend_and_choose(CHUNKS - 2, 0, None, True)
            prepare(CHUNKS - 2, False, True, CHUNKS * BC)
            count_places(CHUNKS - 1, CHUNKS * BC)

            pe.wait_ge(table_ready, 1)
            pe.wait_ge(low_ready, CHUNKS * PIECES)
            pe.wait_ge(w2_in, 16 * CHUNKS)

            most = (EXPERTS - 1) * HID
            carried = [pe.alloc_register(f"weights_at{n}") for n in range(2)]

            def weights_at(t):
                return pe.value_load(tile_weights[0:1, bass.ds(t, 1)], min_val=0, max_val=most)

            def carry(t, n):
                pe.reg_load(carried[n], tile_weights[0:1, bass.ds(t, 1)])

            def transpose_xs(t, n):
                pe.wait_ge(xs_in[n % RING], (t + 1 - (n % RING)) * (16 // RING) + (16 - 16 // RING))
                nc.tensor.transpose(bank[6][:, 0:P], xs[:, n % RING, 0:D],
                                    ident[:, :]).then_inc(xs_transposed, 1)

            def product(to, n, which, at):
                high, low = w_high[which][:, bass.ds(at, HID)], w_low[which][:, bass.ds(at, HID)]
                mm(to, xsT[:, n % 2, 0, :], high, start=True, stop=False)
                mm(to, xsT[:, n % 2, 0, :], low, start=False, stop=False)
                return mm(to, xsT[:, n % 2, 1, :], high, start=False, stop=True)

            def gate(t, n, at):
                pe.wait_ge(xsT_low, t + 1)
                product(bank[n % 2][:, :], n, 0, at).then_inc(gate_done, 1)

            def up(n, at):
                product(bank[2 + n % 2][:, :], n, 1, at).then_inc(up_done, 1)

            def step(j, n, at, rest):
                if rest > 1:
                    gate(j + 1, n + 1, at[n + 1])
                pe.wait_ge(hid_ready, j + 1)
                for half, transposed in ((0, low_transposed), (1, high_transposed)):
                    for k in range(HK // 2):
                        at_k = (half * HK // 2 + k) * P
                        last = nc.tensor.transpose(bank[4 + half][:, k * P:(k + 1) * P],
                                                   hid[:, n % 2, at_k:at_k + P], ident[:, :])
                    last.then_inc(transposed, 1)
                if rest > 2:
                    transpose_xs(j + 2, n + 2)
                if rest > 1:
                    up(n + 1, at[n + 1])
                if rest > 2:
                    if n + 2 <= RING:
                        at.append(weights_at(j + 2))
                    if n + 2 >= RING:
                        carry(j + 2, n + 2 - RING)
                for k in range(HK):
                    if k == 0:
                        pe.wait_ge(hidT_low, j + 1)
                        pe.wait_ge(y_ready, j + 1)
                    elif k == HK // 2:
                        pe.wait_ge(hidT_high, j + 1)
                    last = mm(bank[7][:, 0:D], hidT[:, k * P:(k + 1) * P],
                              w2_sb[:, bass.ds(at[n] + k * D, D)], start=(k == 0), stop=(k == HK - 1))
                last.then_inc(down_done, 1)

            transpose_xs(0, 0)
            pe.wait_ge(xsT_low, 1)
            transpose_xs(1, 1)
            carry(0, 0)
            carry(1, 1)
            first_at = weights_at(0)
            gate(0, 0, first_at)
            up(0, first_at)

            def taken():
                return [pe.snap(r, min_val=0, max_val=most) for r in carried]

            with pe.Fori(0, AHEAD // RING) as i:
                at = taken()
                for n in range(RING):
                    step(i * RING + n, n, at, RING)
            at = taken()
            for n in range(RING):
                step(AHEAD + n, n, at, RING - n)


def kernel(x, L0_tok_conv_w, L0_attn_W_qk, L0_attn_W_v, L0_attn_b_v, L0_ffn_Wr, L0_ffn_br, L0_ffn_Wgate,
           L0_ffn_bgate, L0_ffn_W1, L0_ffn_W3, L0_ffn_W2):
    import numpy as np
    import concourse.bacc as bacc
    from concourse.bass_utils import run_bass_kernel_spmd

    lay = np.ascontiguousarray
    arrays = {
        "ids": lay(np.asarray(x).reshape(TILES_IN, P).T),
        "embedding": lay(np.asarray(L0_tok_conv_w).transpose(1, 2, 0).reshape(VOCAB, TAPS * D)),
        "w_qk": lay(L0_attn_W_qk),
        "w_v_t": lay(np.asarray(L0_attn_W_v).T),
        "b_v": lay(L0_attn_b_v),
        "w_route": lay(L0_ffn_Wr),
        "w_gate": lay(np.asarray(L0_ffn_Wgate).transpose(1, 0, 2).reshape(D, EXPERTS)),
        "b_route": lay(L0_ffn_br),
        "b_gate": lay(np.asarray(L0_ffn_bgate).reshape(EXPERTS)),
        "w1": lay(np.asarray(L0_ffn_W1).transpose(1, 0, 2).reshape(D, EXPERTS * HID)),
        "w3": lay(np.asarray(L0_ffn_W3).transpose(1, 0, 2).reshape(D, EXPERTS * HID)),
        "w2": lay(np.asarray(L0_ffn_W2).reshape(EXPERTS, HK, P, D).transpose(2, 0, 1, 3).reshape(P, -1)),
    }
    nc = bacc.Bacc("TRN2", target_bir_lowering=False, num_devices=1)
    args = [nc.dram_tensor(name, a.shape, mybir.dt.from_np(a.dtype), kind="ExternalInput").ap()
            for name, a in arrays.items()]
    out = nc.dram_tensor("out", [BATCHES, SEQ, D], F32, kind="ExternalOutput").ap()
    tower_kernel(nc, *args, out)
    return run_bass_kernel_spmd(nc, [arrays], core_ids=[0]).results[0]["out"]
```

```python
from contextlib import ExitStack

import concourse.bass as bass
from concourse import mybir

F32 = mybir.dt.float32
F32R = mybir.dt.float32r
BF16 = mybir.dt.bfloat16
I32 = mybir.dt.int32
ALU = mybir.AluOpType
ACT = mybir.ActivationFunctionType
AX = mybir.AxisListType

P = 128
D = 128
TAPS = 3
VOCAB = 8000
BATCHES, SEQ = 16, 256
TOKENS = BATCHES * SEQ
TILES_IN = TOKENS // P
CHUNKS = 8
TC = TILES_IN // CHUNKS
BC = BATCHES // CHUNKS
GROUPS, PER_GROUP = 4, 4
EXPERTS = GROUPS * PER_GROUP
SETS = GROUPS + 1
SLOTS = 4
HID = 512
HK = HID // P
KEEP = 0.9
EPS = 1e-5
SCALE = float(D) ** -0.5
SLOPE = 0.5
MASKED = -3.0e38

REC = D + EXPERTS + 1
REGION = TOKENS + P
TILES = 144
SPARE = TILES - TOKENS * SLOTS // P
SENT_ROWS = EXPERTS * REGION + SPARE * P
RING = 4
AHEAD = TILES - RING

PART = EXPERTS * HID // CHUNKS
PIECES = 2 * PART // 512
assert PIECES == 4 and TC == 4
LAST_CHUNKS = 8
FRONT = (CHUNKS - 2) // 2
VECTOR_PER_PASS = 2 * (26 + 4 * BC)


def tower_kernel(nc, ids, embedding, w_qk, w_v_t, b_v, w_route, w_gate, b_route, b_gate, w1, w3, w2, out):
    ctx = ExitStack()
    with ctx:
        def sb(name, shape, dt=F32):
            return ctx.enter_context(nc.sbuf_tensor(name, shape, dt))

        def sem(name):
            return ctx.enter_context(nc.semaphore(name))

        bank = [ctx.enter_context(nc.psum_tensor(f"bank{n}", [P, 512], F32)) for n in range(8)]

        sent = nc.dram_tensor("sent", [SENT_ROWS, REC], F32, kind="Internal").ap()
        sums = [nc.dram_tensor(f"sums{n}", [TOKENS + P, D], F32, kind="Internal").ap() for n in range(2)]

        START = -(-nc.sbuf_base // 32) * 32
        WEIGHTS = EXPERTS * HID
        sb("weights_space", [P, 4 * WEIGHTS + TC * P])

        def within(name, floats_in, shape, dt=F32):
            return nc.alloc_sbuf_tensor_at(name, shape, dt, offset=START + 4 * floats_in)

        w_high = [within(f"w{n}_high", i * WEIGHTS, [P, WEIGHTS], F32R) for i, n in enumerate((1, 3))]
        w_low = [within(f"w{n}_low", (2 + i) * WEIGHTS, [P, WEIGHTS], F32R) for i, n in enumerate((1, 3))]
        w_raw = [within(f"w{n}_raw", (2 + i) * WEIGHTS, [P, WEIGHTS]) for i, n in enumerate((1, 3))]
        LATE_FROM = EXPERTS * HID * (CHUNKS - 2) // CHUNKS
        late = [i * WEIGHTS + LATE_FROM for i in range(2)]
        assert 2 * 2 * TC * D == WEIGHTS - LATE_FROM and TC * D + 3 * 2 * SEQ == WEIGHTS - LATE_FROM

        ident = sb("ident", [P, P])
        from_before = sb("from_before", [P, P])
        from_after = sb("from_after", [P, P])
        last_to_first = sb("last_to_first", [P, P])
        first_to_last = sb("first_to_last", [P, P])
        earlier = sb("earlier", [P, P], BF16)
        ones = sb("ones", [P, P], BF16)
        position_bias = sb("position_bias", [P, 3 * P])
        eps = sb("eps", [P, 1])
        zeros = sb("zeros", [P, D])
        pad_rows = sb("pad_rows", [P, REC])
        token_number = sb("token_number", [P, TILES_IN])
        region_start = sb("region_start", [P, EXPERTS])
        tile_number = sb("tile_number", [1, TILES])
        ones_row = sb("ones_row", [1, EXPERTS])

        ids_sb = sb("ids_sb", [P, TILES_IN], I32)
        wqk_sb = sb("wqk_sb", [P, D])
        wvt_sb = sb("wvt_sb", [P, D])
        bv_sb = sb("bv_sb", [P, D])
        router_w = sb("router_w", [P, SETS * PER_GROUP])
        router_b = sb("router_b", [P, SETS * PER_GROUP])
        w2_sb = sb("w2_sb", [P, EXPERTS * HID])

        taps_of = sb("taps", [P, 2, TC, TAPS * D])
        assert TC * TAPS * D <= WEIGHTS - LATE_FROM == 2 * PART
        taps_at = [within(f"taps{c}", at, [P, TC, TAPS * D]) for c, at in enumerate(
            (2 * WEIGHTS + late[0], 2 * WEIGHTS + late[1], 2 * PART, WEIGHTS + 2 * PART))]
        taps_at += [taps_of[:, c % 2] for c in range(len(taps_at), CHUNKS)]
        EARLY = 6
        h_of = within("h", late[0], [P, 2, TC, D])
        stats = sb("stats", [P, 2, TC, 6])
        half_sums = sb("half_sums", [P, 4, 2, TC])
        mean = sb("mean", [P, 2, TC])
        var = sb("var", [P, 2, TC])
        std = sb("std", [P, 2, TC])
        rstd = sb("rstd", [P, 2, TC])
        shift = sb("shift", [P, TC])
        xn = within("xn", late[1], [P, TC, D])
        xT = within("xT", late[1] + TC * D, [P, 2, SEQ])
        qT = within("qT", late[1] + TC * D + 2 * SEQ, [P, 2, SEQ])
        v = within("v", late[1] + TC * D + 4 * SEQ, [P, 2, SEQ])
        attention_work = sb("attention_work", [P, 3, 2, 3 * P])
        scores, probs, pT = (attention_work[:, n, :, :] for n in range(3))
        neg_max = sb("neg_max", [P, 2, 2])
        row_sum = sb("row_sum", [P, 2, 2])
        row_inv = sb("row_inv", [P, 2, 2])
        h1_of = within("h1", late[0] + 2 * TC * D, [P, 2, TC, D])
        x2 = sb("x2", [P, TC, D])
        rows_of = sb("rows", [P, 2, TC, REC])
        x2T = within("x2T", 4 * WEIGHTS, [P, TC * P])

        NS = TC * SETS
        logits = sb("logits", [P, NS, PER_GROUP])
        set_max = sb("set_max", [P, NS])
        shifted = sb("shifted", [P, NS, PER_GROUP])
        choice = sb("choice", [P, NS, PER_GROUP])
        set_sum = sb("set_sum", [P, NS])
        set_inv = sb("set_inv", [P, NS])
        beats = sb("beats", [P, NS, 6])
        part = sb("part", [P, NS, PER_GROUP])
        rank = sb("rank", [P, NS, PER_GROUP])
        is_first = sb("is_first", [P, NS, PER_GROUP])
        is_second = sb("is_second", [P, NS, PER_GROUP])
        p_first = sb("p_first", [P, NS])
        p_second = sb("p_second", [P, NS])
        both = sb("both", [P, NS])
        kept_sum = sb("kept_sum", [P, NS])
        kept = sb("kept", [P, NS])
        kept_inv = sb("kept_inv", [P, NS])
        share = sb("share", [P, TC, SETS, PER_GROUP])
        group_share = sb("group_share", [P, TC, GROUPS])
        far = sb("far", [P, NS, PER_GROUP])
        group_slot = sb("group_slot", [P, TC, GROUPS])
        slot = sb("slot", [P, TC, GROUPS, PER_GROUP])
        chosen = sb("chosen", [P, TC, EXPERTS], BF16)
        next_row = sb("next_row", [P, EXPERTS])
        place = sb("place", [P, TC, EXPERTS])
        place_of = sb("place_of", [P, SLOTS, TC, EXPERTS])
        place_in = sb("place_in", [P, SLOTS, TC])
        send_to_of = sb("send_to", [P, 2, SLOTS, TC], I32)

        count = sb("count", [1, EXPERTS])
        count_i = sb("count_i", [1, EXPERTS], I32)
        tiles_i = sb("tiles_i", [1, EXPERTS], I32)
        tiles_of = sb("tiles_of", [1, EXPERTS])
        tiles_to = sb("tiles_to", [1, EXPERTS])
        passed = attention_work[0:1, :, :, :].rearrange("p a b n -> p (a b n)")[:, 0:TILES * EXPERTS].rearrange(
            "p (t e) -> p t e", e=EXPERTS)
        x2_space = x2[0:1, :, :].rearrange("p t n -> p (t n)")
        tile_expert, tile_in_region, tile_region = (x2_space[:, n * TILES:(n + 1) * TILES] for n in range(3))
        tiles_before = position_bias[0:1, 0:TILES]
        tile_row = sb("tile_row", [1, TILES], I32)
        tile_column = sb("tile_column", [1, TILES], I32)
        tile_weights = sb("tile_weights", [1, TILES], I32)
        pad_start = sb("pad_start", [1, EXPERTS], I32)

        xsT = within("xsT", 4 * WEIGHTS, [P, 2, 2, P], F32R)
        assert TC == 4 and RING <= TC and 5 * HID + RING * D <= 2 * TC * TAPS * D
        xs = rows_of[:, 0]
        taps_space = taps_of[:, :, :, :].rearrange("p a t n -> p (a t n)")
        gated = taps_space[:, 0:2 * HID].rearrange("p (r n) -> p r n", r=2)
        hid = taps_space[:, 2 * HID:4 * HID].rearrange("p (r n) -> p r n", r=2)
        hidT = taps_space[:, 4 * HID:5 * HID]
        y = taps_space[:, 5 * HID:5 * HID + RING * D].rearrange("p (r n) -> p r n", r=RING)
        add_to = sb("add_to", [P, RING], I32)

        ids_in = sem("ids_in")
        front_weights_in = sem("front_weights_in")
        weights_in = [sem(f"weights_in{n}") for n in range(2)]
        w2_in = sem("w2_in")
        high_ready = sem("high_ready")
        low_ready = sem("low_ready")
        pool_step = sem("pool_step")
        shifts_ready = sem("shifts_ready")
        constants_ready = sem("constants_ready")
        gathered = [sem(f"gathered{n}") for n in range(EARLY)]
        send_begun = sem("send_begun")
        embedded = sem("embedded")
        h_ready = sem("h_ready")
        stats_ready = sem("stats_ready")
        var_ready = sem("var_ready")
        std_ready = sem("std_ready")
        shift_ready = sem("shift_ready")
        xn_ready = sem("xn_ready")
        xn_transposed = sem("xn_transposed")
        xT_ready = sem("xT_ready")
        q_done = sem("q_done")
        v_done = sem("v_done")
        qT_ready = sem("qT_ready")
        v_ready = sem("v_ready")
        scores_done = sem("scores_done")
        max_ready = sem("max_ready")
        probs_ready = sem("probs_ready")
        probs_transposed = sem("probs_transposed")
        pT_ready = sem("pT_ready")
        pv_done = sem("pv_done")
        h1_ready = sem("h1_ready")
        h1_stored = [sem(f"h1_stored{n}") for n in range(2)]
        x2_ready = sem("x2_ready")
        x2_transposed = sem("x2_transposed")
        x2T_ready = sem("x2T_ready")
        logits_done = sem("logits_done")
        shifted_ready = sem("shifted_ready")
        choice_ready = sem("choice_ready")
        chosen_ready = sem("chosen_ready")
        places_done = sem("places_done")
        rows_copied = sem("rows_copied")
        rows_ready = sem("rows_ready")
        rows_sent = [sem(f"rows_sent{n}") for n in range(2)]
        vector_step = sem("vector_step")
        regions_ready = sem("regions_ready")
        table_ready = sem("table_ready")
        zeros_stored = sem("zeros_stored")
        pads_stored = sem("pads_stored")
        xs_in = [sem(f"xs_in{n}") for n in range(RING)]
        xs_transposed = sem("xs_transposed")
        xsT_high = sem("xsT_high")
        xsT_low = sem("xsT_low")
        gate_done = sem("gate_done")
        up_done = sem("up_done")
        gated_ready = sem("gated_ready")
        hid_ready = sem("hid_ready")
        low_transposed = sem("low_transposed")
        high_transposed = sem("high_transposed")
        hidT_low = sem("hidT_low")
        hidT_high = sem("hidT_high")
        down_done = sem("down_done")
        y_ready = sem("y_ready")
        y_free = sem("y_free")
        added = [sem(f"added{n}") for n in range(2)]
        sums_in = [sem(f"sums_in{n}") for n in range(LAST_CHUNKS)]
        out_ready = sem("out_ready")
        out_stored = sem("out_stored")


        sum_parts = [w[:, 0:TILES_IN * D].rearrange("p (c t n) -> p c t n", c=LAST_CHUNKS, n=D) for w in w_raw]

        def by_chunk(rows):
            return rows.rearrange("(c p t) n -> c p t n", p=P, c=LAST_CHUNKS)

        def older(c, b, n=BC):
            return c * n + max(b - 1, 0)

        block = ctx.enter_context(nc.Block())

        @block.sync
        def _(sp):
            sp.dma_start(ids_sb[:, :], ids).then_inc(ids_in, 16)
            for par in range(2):
                sp.sem_inc(h1_stored[par], 16)
            for dst, src in (
                (wqk_sb[:, :], w_qk), (wvt_sb[:, :], w_v_t), (bv_sb[:, :], b_v.partition_broadcast(P)),
                (router_w[:, 0:EXPERTS], w_gate), (router_w[:, EXPERTS:], w_route),
                (router_b[:, 0:EXPERTS], b_gate.partition_broadcast(P)),
                (router_b[:, EXPERTS:], b_route.partition_broadcast(P)),
            ):
                sp.dma_start(dst, src).then_inc(front_weights_in, 16)
            def load_weights(c, par):
                at = bass.ds(c * PART, PART)
                for dst, src, landed in ((w_raw[0], w1, weights_in[par]), (w_raw[1], w3, weights_in[par]),
                                         (w2_sb, w2, w2_in)):
                    sp.dma_start(dst[:, at], src[:, at]).then_inc(landed, 16)

            def store_h1(c, par):
                sp.wait_ge(h1_ready, c * BC + BC)
                sp.dma_start(sums[0][bass.ds(c * (TC * P), TC * P), :].rearrange("(t p) n -> p t n", p=P),
                             h1_of[:, par]).then_inc(h1_stored[par], 16)

            for c in range(3):
                sp.wait_ge(gathered[c], 16 * TC)
            load_weights(0, 0)
            sp.wait_ge(constants_ready, 1)
            sp.dma_start(sums[1].rearrange("(t p) n -> p t n", p=P),
                         zeros[:, :].unsqueeze(1).broadcast_to([P, TILES_IN + 1, D])).then_inc(zeros_stored, 16)
            sp.dma_start(sums[0][TOKENS:, :], zeros[:, :]).then_inc(zeros_stored, 16)
            sp.dma_start(sent[EXPERTS * REGION:, :].rearrange("(t p) n -> p t n", p=P),
                         pad_rows[:, :].unsqueeze(1).broadcast_to([P, SPARE, REC])).then_inc(pads_stored, 16)
            with sp.Fori(0, FRONT) as i:
                for par in range(2):
                    store_h1(i * 2 + par, par)
                    load_weights(i * 2 + (par + 1), 1 - par)
            store_h1(CHUNKS - 2, 0)
            load_weights(CHUNKS - 1, 1)
            store_h1(CHUNKS - 1, 1)
            sp.wait_ge(regions_ready, 1)
            for e in range(EXPERTS):
                start = sp.value_load(pad_start[0:1, e:e + 1], min_val=0, max_val=EXPERTS * REGION - P)
                sp.dma_start(sent[bass.ds(start, P), :], pad_rows[:, :]).then_inc(pads_stored, 16)
            sp.wait_ge(table_ready, 1)

            def row_of(t):
                return sp.value_load(tile_row[0:1, bass.ds(t, 1)], min_val=0, max_val=SENT_ROWS - P)

            def load(row, ring):
                sp.dma_start(xs[:, ring, :], sent[bass.ds(row, P), :]).then_inc(xs_in[ring], 16)

            first_rows = [row_of(n) for n in range(RING)]
            sp.wait_ge(pads_stored, 16 * (EXPERTS + 1))
            for par in range(2):
                sp.wait_ge(rows_sent[par], 16 * CHUNKS // 2 * TC * SLOTS)
            for n in range(RING):
                load(first_rows[n], n)
            with sp.Fori(0, AHEAD // RING) as i:
                for n in range(RING):
                    sp.wait_ge(hid_ready, i * RING + n + 1)
                    load(row_of(i * RING + n + RING), n)
            sp.wait_ge(added[0], 16 * TILES // 2)
            sp.wait_ge(added[1], 16 * TILES // 2)
            for c in range(LAST_CHUNKS):
                for n in range(2):
                    sp.dma_start(sum_parts[n][:, c], by_chunk(sums[n][0:TOKENS, :])[c]).then_inc(sums_in[c], 16)
            sp.wait_ge(zeros_stored, 32)
            for par in range(2):
                sp.wait_ge(h1_stored[par], 16 * CHUNKS // 2 + 16)

        @block.gpsimd
        def _(pool):
            steps = [0]

            def step(ins):
                steps[0] += 1
                ins.then_inc(pool_step, 1)

            def settle():
                pool.wait_ge(pool_step, steps[0])

            def gather(c):
                if c >= EARLY:
                    pool.wait_ge(embedded, (c - 1) * BC)
                for t in range(c * TC, c * TC + TC):
                    nc.gpsimd.indirect_dma_start(
                        out=taps_at[c][:, t % TC, :], out_offset=None, in_=embedding[:, :],
                        in_offset=bass.IndirectOffsetOnAxis(ap=ids_sb[:, t:t + 1], axis=0)
                    ).then_inc(gathered[c if c < EARLY else c - 2], 16)

            def send(par):
                for s in range(SLOTS):
                    for t in range(TC):
                        nc.gpsimd.indirect_dma_start(
                            out=sent[:, :], out_offset=bass.IndirectOffsetOnAxis(ap=send_to_of[:, par, s, t:t + 1], axis=0),
                            in_=rows_of[:, par, t, :], in_offset=None).then_inc(rows_sent[par], 16)

            for m in (ident, from_before, from_after, last_to_first, first_to_last):
                step(nc.gpsimd.memset(m[:, :], 0.0))
            step(nc.gpsimd.memset(eps[:, :], EPS))
            pool.wait_ge(ids_in, 16)
            settle()
            gather(0)
            for m, base, per_partition in ((ident, 0, -1), (from_before, -1, -1), (from_after, 1, -1),
                                           (last_to_first, P * (P - 1), -P), (first_to_last, -(P - 1), P)):
                step(nc.gpsimd.affine_select(out=m[:, :], in_=m[:, :], pattern=[[1, P]],
                                             compare_op=ALU.not_equal, fill=1.0, base=base,
                                             channel_multiplier=per_partition))
            settle()
            pool.sem_inc(shifts_ready, 1)
            gather(1)
            step(nc.gpsimd.memset(ones[:, :], 1.0))
            settle()
            step(nc.gpsimd.affine_select(out=earlier[:, :], in_=ones[:, :], pattern=[[1, P]],
                                         compare_op=ALU.is_gt, fill=0.0, base=0, channel_multiplier=-1))
            step(nc.gpsimd.iota(position_bias[:, 0:P], pattern=[[1, P]], base=0, channel_multiplier=-1,
                                allow_small_or_imprecise_dtypes=True))
            step(nc.gpsimd.iota(position_bias[:, P:], pattern=[[1, 2 * P]], base=-P, channel_multiplier=-1,
                                allow_small_or_imprecise_dtypes=True))
            settle()
            step(nc.gpsimd.tensor_scalar(position_bias[:, :], position_bias[:, :], SLOPE, None, ALU.mult))
            settle()
            for cols, base in ((position_bias[:, 0:P], 0), (position_bias[:, P:], P)):
                step(nc.gpsimd.affine_select(out=cols, in_=cols, pattern=[[-1, cols.shape[1]]],
                                             compare_op=ALU.is_ge, fill=MASKED, base=base, channel_multiplier=1))
            step(nc.gpsimd.memset(zeros[:, :], 0.0))
            step(nc.gpsimd.memset(pad_rows[:, 0:REC - 1], 0.0))
            step(nc.gpsimd.iota(pad_rows[:, REC - 1:], pattern=[[0, 1]], base=TOKENS, channel_multiplier=1,
                                allow_small_or_imprecise_dtypes=True))
            step(nc.gpsimd.iota(token_number[:, :], pattern=[[P, TILES_IN]], base=0, channel_multiplier=1,
                                allow_small_or_imprecise_dtypes=True))
            for m in (region_start, next_row):
                step(nc.gpsimd.iota(m[:, :], pattern=[[REGION, EXPERTS]], base=0, channel_multiplier=0,
                                    allow_small_or_imprecise_dtypes=True))
            step(nc.gpsimd.iota(tile_number[:, :], pattern=[[1, TILES]], base=0, channel_multiplier=0,
                                allow_small_or_imprecise_dtypes=True))
            step(nc.gpsimd.memset(ones_row[:, :], 1.0))
            settle()
            pool.sem_inc(constants_ready, 1)

            def next_send(c, par):
                pool.wait_ge(rows_ready, c + 2)
                pool.sem_inc(send_begun, 1)
                send(par)

            for c in range(2, EARLY):
                gather(c)
            for c in range(4):
                if EARLY <= c + 4 < CHUNKS:
                    gather(c + 4)
                next_send(c, c % 2)
            with pool.Fori(2, CHUNKS // 2) as i:
                for par in range(2):
                    next_send(i * 2 + par, par)

            pool.sem_inc(y_free, 2)
            pool.wait_ge(zeros_stored, 32)
            for par in range(2):
                pool.wait_ge(h1_stored[par], 16 * CHUNKS // 2 + 16)

            def add(t, n, added_before):
                pool.wait_ge(y_ready, t + 2)
                if added_before is not None:
                    pool.wait_ge(added[n % 2], added_before)
                pool.sem_inc(y_free, 1)
                nc.gpsimd.indirect_dma_start(
                    out=sums[n % 2][:, :], out_offset=bass.IndirectOffsetOnAxis(ap=add_to[:, n:n + 1], axis=0),
                    in_=y[:, n, :], in_offset=None, compute_op=ALU.add).then_inc(added[n % 2], 16)

            for n in range(2):
                add(n, n, None)
            with pool.Fori(0, TILES // RING - 1) as i:
                for n in range(RING):
                    add(i * RING + (n + 2), (n + 2) % RING, i * (16 * RING // 2) + 16 * (n // 2 + 1))
            for n in range(2):
                add(TILES - 2 + n, RING - 2 + n, 16 * (TILES // 2 - 1))

        @block.scalar
        def _(act):

            def copy_xT(c, b):
                act.wait_ge(xn_transposed, c * BC + b + 1)
                act.wait_ge(scores_done, older(c, b))
                nc.scalar.copy(xT[:, b % 2, :], bank[2][:, 0:SEQ]).then_inc(xT_ready, 1)

            def copy_qT(c, b):
                act.wait_ge(q_done, c * BC + b + 1)
                nc.scalar.copy(qT[:, b % 2, :], bank[3][:, 0:SEQ]).then_inc(qT_ready, 1)

            def exponentials(c, b):
                act.wait_ge(max_ready, c * BC + b + 1)
                act.wait_ge(probs_transposed, older(c, b))
                act.wait_ge(h1_ready, older(c, b))
                nc.scalar.activation(probs[:, b % 2, 0:P], scores[:, b % 2, 0:P], ACT.Exp,
                                     bias=neg_max[:, b % 2, 0:1], accum_out=row_sum[:, b % 2, 0:1])
                nc.scalar.activation(probs[:, b % 2, P:], scores[:, b % 2, P:], ACT.Exp,
                                     bias=neg_max[:, b % 2, 1:2], accum_out=row_sum[:, b % 2, 1:2]
                                     ).then_inc(probs_ready, 1)

            def copy_pT(c, b):
                act.wait_ge(probs_transposed, c * BC + b + 1)
                act.wait_ge(pv_done, older(c, b))
                nc.scalar.copy(pT[:, b % 2, :], bank[6][:, 0:3 * P]).then_inc(pT_ready, 1)

            def split(c, par, loads, piece):
                if piece == 0:
                    act.wait_ge(weights_in[par], loads)
                n, at = piece % 2, bass.ds(c * PART + piece // 2 * HID, HID)
                nc.scalar.copy(w_high[n][:, at], w_raw[n][:, at]).then_inc(high_ready, 1)

            def embedding(c, par, b, in_order=False):
                act.wait_ge(embedded, c * BC + (b + 1 if in_order else BC))
                nc.scalar.copy(h_of[:, par, 2 * b:2 * b + 2, :].rearrange("p t n -> p (t n)"),
                               bank[b][:, 0:SEQ]).then_inc(h_ready, 1)

            def roots(which, count):
                act.wait_ge(var_ready, count)
                nc.scalar.activation(std[:, which, :], var[:, which, :], ACT.Sqrt, bias=eps[:, 0:1],
                                     scale=0.25).then_inc(std_ready, 1)

            def copies(c, b):
                copy_xT(c, b)
                copy_qT(c, b)

            def attend_and_choose(k, par, loads, sent_before, a_too, b_too):
                if b_too:
                    exponentials(k + 1, 0)
                if sent_before is not None:
                    act.wait_ge(rows_sent[par], sent_before)
                act.wait_ge(x2_ready, k + 1)
                nc.scalar.copy(rows_of[:, par, :, 0:D], x2[:, :, :]).then_inc(rows_copied, 1)
                if b_too:
                    copy_pT(k + 1, 0)
                if loads is not None:
                    split(k, par, loads, 0)
                if b_too:
                    exponentials(k + 1, 1)
                act.wait_ge(shifted_ready, k + 1)
                nc.scalar.activation(choice[:, :, :], shifted[:, :, :], ACT.Exp).then_inc(choice_ready, 1)
                if a_too:
                    act.wait_ge(h1_ready, k * BC + BC)
                    for b in range(BC):
                        embedding(k + 2, par, b)
                if b_too:
                    copy_pT(k + 1, 1)
                if loads is not None:
                    for piece in range(1, PIECES):
                        split(k, par, loads, piece)

            def prepare(k, par, a_too):
                roots(slice(0, 2) if a_too else slice(1, 2), k + 3)
                if a_too:
                    copies(k + 2, 0)
                act.wait_ge(shift_ready, k + 2)
                for t in range(TC):
                    last = nc.scalar.activation(x2[:, t, :], h1_of[:, 1 - par, t, :], ACT.Identity,
                                                bias=shift[:, t:t + 1], scale=rstd[:, 1, t:t + 1])
                last.then_inc(x2_ready, 1)
                act.wait_ge(x2_transposed, k + 2)
                act.wait_ge(logits_done, k + 1)
                nc.scalar.copy(x2T[:, :], bank[0][:, :]).then_inc(x2T_ready, 1)
                if a_too:
                    copies(k + 2, 1)

            act.wait_ge(shifts_ready, 1)
            for b in range(BC):
                embedding(0, 0, b, in_order=True)
            roots(slice(0, 1), 1)
            for b in range(BC):
                embedding(1, 1, b, in_order=True)
            for b in range(BC):
                copies(0, b)
            for b in range(BC):
                exponentials(0, b)
                copy_pT(0, b)
            prepare(-1, 1, True)
            per_half = 16 * TC * SLOTS
            for k in range(2):
                attend_and_choose(k, k, 32, None, True, True)
                prepare(k, k, True)
            with act.Fori(0, FRONT - 1) as i:
                for par in range(2):
                    k = i * 2 + (2 + par)
                    attend_and_choose(k, par, i * 32 + 64, i * per_half + per_half, True, True)
                    prepare(k, par, True)
            attend_and_choose(CHUNKS - 2, 0, None, FRONT * per_half, False, True)
            prepare(CHUNKS - 2, 0, False)
            attend_and_choose(CHUNKS - 1, 1, None, FRONT * per_half, False, False)
            act.wait_ge(x2_ready, CHUNKS)
            for par in range(2):
                act.wait_ge(h1_stored[par], 16 * CHUNKS // 2 + 16)
            act.wait_ge(scores_done, CHUNKS * BC)
            act.wait_ge(pv_done, CHUNKS * BC)
            for c in (CHUNKS - 2, CHUNKS - 1):
                for piece in range(PIECES):
                    split(c, c % 2, 16 * CHUNKS, piece)

            def copy_xsT(t, ring):
                act.wait_ge(xs_transposed, t + 1)
                nc.scalar.copy(xsT[:, ring % 2, 0, :], bank[6][:, 0:P]).then_inc(xsT_high, 1)

            def silu(t, ring):
                act.wait_ge(gate_done, t + 1)
                nc.scalar.activation(gated[:, ring % 2, :], bank[ring % 2][:, :], ACT.Silu).then_inc(gated_ready, 1)

            def step(j, n, rest):
                if rest > 1:
                    silu(j + 1, n + 1)
                act.wait_ge(low_transposed, j + 1)
                nc.scalar.copy(hidT[:, 0:HID // 2], bank[4][:, 0:HID // 2]).then_inc(hidT_low, 1)
                if rest > 2:
                    copy_xsT(j + 2, n + 2)

            copy_xsT(0, 0)
            copy_xsT(1, 1)
            silu(0, 0)
            with act.Fori(0, AHEAD // RING) as i:
                for n in range(RING):
                    step(i * RING + n, n, RING)
            for n in range(RING):
                step(AHEAD + n, n, RING - n)

            for c in range(LAST_CHUNKS):
                act.wait_ge(out_ready, c + 1)
                act.dma_start(by_chunk(out.rearrange("b s n -> (b s) n"))[c], sum_parts[0][:, c]).then_inc(out_stored, 16)
            act.wait_ge(out_stored, 16 * LAST_CHUNKS)

        @block.vector
        def _(dve):
            steps = [0]
            before = [0]

            def link(ins):
                steps[0] += 1
                ins.then_inc(vector_step, 1)
                dve.wait_ge(vector_step, before[0] + steps[0])

            def begin(ins):
                steps[0] += 1
                ins.then_inc(vector_step, 1)
                return steps[0]

            def settle(step):
                dve.wait_ge(vector_step, before[0] + step)

            def cells(ap, shape):
                return ap.broadcast_to(shape)

            tt, ts, stt = nc.vector.tensor_tensor, nc.vector.tensor_scalar, nc.vector.scalar_tensor_tensor

            def values_and_scores(c, b):
                dve.wait_ge(v_done, c * BC + b + 1)
                dve.wait_ge(pv_done, older(c, b))
                tt(v[:, b % 2, :].rearrange("p (t n) -> p t n", t=2),
                   bank[5][:, 0:SEQ].rearrange("p (t n) -> p t n", t=2),
                   cells(bv_sb[:, :].unsqueeze(1), [P, 2, D]), ALU.add).then_inc(v_ready, 1)
                dve.wait_ge(scores_done, c * BC + b + 1)
                dve.wait_ge(probs_ready, older(c, b))
                link(stt(scores[:, b % 2, :], bank[4][:, 0:3 * P], SCALE, position_bias[:, :],
                         ALU.mult, ALU.add))
                nc.vector.tensor_reduce(neg_max[:, b % 2, 0:1], scores[:, b % 2, 0:P], AX.X, ALU.max, negate=True)
                nc.vector.tensor_reduce(neg_max[:, b % 2, 1:2], scores[:, b % 2, P:], AX.X, ALU.max,
                                        negate=True).then_inc(max_ready, 1)

            def residual(c, par, b, stored):
                h, h1 = h_of[:, par], h1_of[:, par]
                if b == 0 and stored is not None:
                    dve.wait_ge(h1_stored[par], stored + 16)
                dve.wait_ge(probs_ready, c * BC + b + 1)
                link(nc.vector.reciprocal(row_inv[:, b % 2, :], row_sum[:, b % 2, :]))
                dve.wait_ge(pv_done, c * BC + b + 1)
                added = [begin(stt(h1[:, 2 * b + t, :], bank[7][:, t * D:(t + 1) * D], row_inv[:, b % 2, t:t + 1],
                                   h[:, 2 * b + t, :], ALU.mult, ALU.add)) for t in range(2)]
                for t in range(2):
                    settle(added[t])
                    last = nc.vector.bn_stats(stats[:, 1, 2 * b + t, :], h1[:, 2 * b + t, :])
                last.then_inc(h1_ready, 1)

            def moments(which, meanwhile=None):
                summed, apart, squares, square = (half_sums[:, n, which, :] for n in range(4))
                of = stats[:, which]
                tt(summed, of[:, :, :, 1], of[:, :, :, 4], ALU.add)
                tt(apart, of[:, :, :, 1], of[:, :, :, 4], ALU.subtract)
                halves = begin(tt(squares, of[:, :, :, 2], of[:, :, :, 5], ALU.add))
                if meanwhile is not None:
                    meanwhile()
                settle(halves)
                ts(mean[:, which, :], summed, 0.5, None, ALU.mult)
                link(tt(square, apart, apart, ALU.mult))
                stt(var[:, which, :], squares, 4.0 / D, square, ALU.mult, ALU.add).then_inc(var_ready, 1)

            all4 = [P, NS, PER_GROUP]

            def shifted_logits(c):
                dve.wait_ge(logits_done, c + 1)
                link(tt(logits[:, :, :].rearrange("p (t g) e -> p t (g e)", g=SETS),
                        bank[3][:, 0:TC * SETS * PER_GROUP].rearrange("p (t n) -> p t n", t=TC),
                        cells(router_b[:, :].unsqueeze(1), [P, TC, SETS * PER_GROUP]), ALU.add))
                link(nc.vector.tensor_reduce(set_max[:, :], logits[:, :, :], AX.X, ALU.max))
                tt(shifted[:, :, :], logits[:, :, :], cells(set_max[:, :].unsqueeze(2), all4),
                   ALU.subtract).then_inc(shifted_ready, 1)

            def softmaxes(c, new_stats):
                dve.wait_ge(choice_ready, c + 1)
                summed = begin(nc.vector.tensor_reduce(set_sum[:, :], choice[:, :, :], AX.X, ALU.add))
                new_stats(0)
                settle(summed)
                inverted = begin(nc.vector.reciprocal(set_inv[:, :], set_sum[:, :]))
                new_stats(1)
                settle(inverted)
                divided = begin(tt(choice[:, :, :], choice[:, :, :], cells(set_inv[:, :].unsqueeze(2), all4), ALU.mult))
                new_stats(2)
                new_stats(3)
                settle(divided)

            def pair(n):
                return beats[:, :, n:n + 1]

            slots = slot[:, :, :, :].rearrange("p t g e -> p t (g e)")

            def choose_first():
                for i, at in ((0, 0), (1, 3), (2, 5)):
                    n = PER_GROUP - 1 - i
                    last = tt(beats[:, :, at:at + n], cells(choice[:, :, i:i + 1], [P, NS, n]),
                              choice[:, :, i + 1:], ALU.is_ge)
                link(last)
                tt(part[:, :, 0:1], pair(0), pair(1), ALU.add)
                tt(part[:, :, 1:2], pair(3), pair(4), ALU.add)
                tt(part[:, :, 2:3], pair(1), pair(3), ALU.add)
                link(tt(part[:, :, 3:4], pair(2), pair(4), ALU.add))
                tt(rank[:, :, 0:1], part[:, :, 0:1], pair(2), ALU.add)
                stt(rank[:, :, 1:2], pair(0), 2.0, part[:, :, 1:2], ALU.add, ALU.subtract)
                stt(rank[:, :, 2:3], part[:, :, 2:3], 1.0, pair(5), ALU.add, ALU.subtract)
                link(tt(rank[:, :, 3:4], part[:, :, 3:4], pair(5), ALU.add))
                link(ts(rank[:, :, 0:1], rank[:, :, 0:1], -1.0, 3.0, ALU.mult, ALU.add))

            def flags():
                ts(far[:, :, :], rank[:, :, :], 2.0, 8.0, ALU.is_ge, ALU.mult)
                ts(is_first[:, :, :], rank[:, :, :], 0.0, None, ALU.is_equal)
                link(ts(is_second[:, :, :], rank[:, :, :], 1.0, None, ALU.is_equal))

            def choose_last():
                far_of = far[:, :, :].rearrange("p (t g) e -> p t g e", g=SETS)
                rank_of = rank[:, :, :].rearrange("p (t g) e -> p t g e", g=SETS)
                stt(group_slot[:, :, :], rank_of[:, :, GROUPS, :], 2.0, far_of[:, :, GROUPS, :], ALU.mult, ALU.add)
                in_group = begin(tt(slot[:, :, :, :], rank_of[:, :, 0:GROUPS, :], far_of[:, :, 0:GROUPS, :], ALU.add))
                tt(part[:, :, :], choice[:, :, :], is_first[:, :, :], ALU.mult)
                picked = begin(tt(shifted[:, :, :], choice[:, :, :], is_second[:, :, :], ALU.mult))
                settle(in_group)
                slotted = begin(tt(slot[:, :, :, :], slot[:, :, :, :],
                                   cells(group_slot[:, :, :].unsqueeze(3), [P, TC, GROUPS, PER_GROUP]), ALU.add))
                settle(picked)
                nc.vector.tensor_reduce(p_first[:, :], part[:, :, :], AX.X, ALU.add)
                summed = begin(nc.vector.tensor_reduce(p_second[:, :], shifted[:, :, :], AX.X, ALU.add))
                settle(slotted)
                ts(chosen[:, :, :], slots, float(SLOTS), None, ALU.is_lt).then_inc(chosen_ready, 1)
                settle(summed)
                link(tt(both[:, :], p_first[:, :], p_second[:, :], ALU.add))
                link(stt(kept[:, :], both[:, :], KEEP, p_second[:, :], ALU.is_le, ALU.mult))

            def weigh_last(c, par, splits):
                tt(shifted[:, :, :], is_second[:, :, :], cells(kept[:, :].unsqueeze(2), all4), ALU.mult)
                summed = begin(stt(kept_sum[:, :], kept[:, :], 1e-9, p_first[:, :], ALU.add, ALU.add))
                if splits:
                    split(c, c, 1)
                settle(summed)
                tt(part[:, :, :], part[:, :, :], shifted[:, :, :], ALU.add)
                inverted = begin(nc.vector.reciprocal(kept_inv[:, :], kept_sum[:, :]))
                dve.wait_ge(rows_copied, c + 1)
                nc.vector.tensor_copy(rows_of[:, par, :, REC - 1], token_number[:, bass.ds(c * TC, TC)])
                settle(inverted)
                shares = share[:, :, :, :].rearrange("p t g e -> p (t g) e")
                link(tt(shares, part[:, :, :], cells(kept_inv[:, :].unsqueeze(2), all4), ALU.mult))
                link(ts(group_share[:, :, :], share[:, :, GROUPS, :], float(GROUPS) ** -0.5, None, ALU.mult))
                tt(rows_of[:, par, :, D:D + EXPERTS].rearrange("p t (g e) -> p t g e", g=GROUPS),
                   share[:, :, 0:GROUPS, :],
                   cells(group_share[:, :, :].unsqueeze(3), [P, TC, GROUPS, PER_GROUP]), ALU.mult)

            def locate(c, par, splits):
                dve.wait_ge(places_done, c + 1)
                link(tt(place[:, :, :], bank[6][:, 0:TC * EXPERTS].rearrange("p (t e) -> p t e", t=TC),
                        cells(next_row[:, :].unsqueeze(1), [P, TC, EXPERTS]), ALU.add))
                tt(next_row[:, :], next_row[:, :], bank[6][:, TC * EXPERTS:(TC + 1) * EXPERTS], ALU.add)
                for s in range(SLOTS):
                    last = stt(place_of[:, s], slots, float(s), place[:, :, :], ALU.is_equal, ALU.mult)
                found = begin(last)
                if splits:
                    split(c, c, 2)
                settle(found)
                link(nc.vector.tensor_reduce(place_in[:, :, :], place_of[:, :, :, :], AX.X, ALU.add))
                nc.vector.tensor_copy(send_to_of[:, par], place_in[:, :, :]).then_inc(rows_ready, 1)

            def split(c, number, piece):
                n, at = piece % 2, bass.ds(c * PART + piece // 2 * HID, HID)
                dve.wait_ge(high_ready, number * PIECES + (piece + 1))
                tt(w_low[n][:, at], w_raw[n][:, at], w_high[n][:, at].bitcast(F32),
                   ALU.subtract).then_inc(low_ready, 1)

            def embedding_stats(c, par, t):
                if t % 2 == 0:
                    dve.wait_ge(h_ready, c * BC + t // 2 + 1)
                return nc.vector.bn_stats(stats[:, 0, t, :], h_of[:, par, t, :])

            def normalise(c, par):
                dve.wait_ge(xn_transposed, c * BC)
                for t in range(TC):
                    last = ts(xn[:, t, :], h_of[:, par, t, :], mean[:, 0, t:t + 1], rstd[:, 0, t:t + 1],
                              ALU.subtract, ALU.mult)
                    if t % 2:
                        last.then_inc(xn_ready, 1)

            def attend_and_choose(k, par, stored, a_too, b_too):
                shifted_logits(k)
                if a_too:
                    split(k, k, 0)
                if b_too:
                    residual(k + 1, 1 - par, 0, stored)
                softmaxes(k, lambda t: embedding_stats(k + 2, par, t) if a_too else None)
                if b_too:
                    residual(k + 1, 1 - par, 1, None)

            def prepare(k, par, a_too, routed):
                dve.wait_ge(h1_ready, k * BC + 2 * BC)
                moments(slice(0, 2) if a_too else slice(1, 2))
                dve.wait_ge(std_ready, k + 3)
                which = slice(0, 2) if a_too else slice(1, 2)
                link(nc.vector.reciprocal(rstd[:, which, :], std[:, which, :]))
                if a_too:
                    normalise(k + 2, par)
                stt(shift[:, :], mean[:, 1, :], -1.0, rstd[:, 1, :], ALU.mult, ALU.mult).then_inc(shift_ready, 1)
                if routed:
                    choose_first()
                    flags()
                    choose_last()
                if a_too:
                    values_and_scores(k + 2, 0)
                if routed:
                    weigh_last(k, par, a_too)
                    locate(k, par, a_too)
                if a_too:
                    values_and_scores(k + 2, 1)
                    if routed:
                        split(k, k, 3)

            dve.sem_inc(rows_ready, 1)
            dve.sem_inc(y_ready, 1)
            for t in range(TC):
                last = embedding_stats(0, 0, t)
            link(last)
            moments(slice(0, 1))
            dve.wait_ge(std_ready, 1)
            link(nc.vector.reciprocal(rstd[:, 0, :], std[:, 0, :]))
            normalise(0, 0)
            dve.wait_ge(constants_ready, 1)
            dve.wait_ge(front_weights_in, 16 * 7)
            for b in range(BC):
                values_and_scores(0, b)
            for t in range(TC):
                embedding_stats(1, 1, t)
            for b in range(BC):
                residual(0, 0, b, None)
            prepare(-1, 1, True, False)
            counted = steps[0]
            with dve.Fori(0, FRONT) as i:
                before[0], steps[0] = i * VECTOR_PER_PASS + counted, 0
                for par in range(2):
                    attend_and_choose(i * 2 + par, par, (i + par) * 16, True, True)
                    prepare(i * 2 + par, par, True, True)
            assert steps[0] == VECTOR_PER_PASS, steps[0]
            before[0], steps[0] = counted + FRONT * VECTOR_PER_PASS, 0
            attend_and_choose(CHUNKS - 2, 0, FRONT * 16, False, True)
            prepare(CHUNKS - 2, 0, False, True)
            attend_and_choose(CHUNKS - 1, 1, None, False, False)
            choose_first()
            flags()
            choose_last()
            weigh_last(CHUNKS - 1, 1, False)
            locate(CHUNKS - 1, 1, False)

            by_tile = [1, TILES, EXPERTS]
            nc.vector.tensor_copy(pad_start[:, :], next_row[0:1, :]).then_inc(regions_ready, 1)
            link(tt(count[:, :], next_row[0:1, :], region_start[0:1, :], ALU.subtract))
            link(ts(count_i[:, :], count[:, :], float(P - 1), None, ALU.add))
            link(ts(tiles_i[:, :], count_i[:, :], P.bit_length() - 1, None, ALU.logical_shift_right))
            link(nc.vector.tensor_copy(tiles_of[:, :], tiles_i[:, :]))
            link(nc.vector.tensor_tensor_scan(tiles_to[:, :], ones_row[:, :], tiles_of[:, :], 0.0,
                                              ALU.mult, ALU.add))
            link(tt(passed[:, :, :], cells(tiles_to[:, :].unsqueeze(1), by_tile),
                    cells(tile_number[:, :].unsqueeze(2), by_tile), ALU.is_le))
            link(nc.vector.tensor_reduce(tile_expert[:, :], passed[:, :, :], AX.X, ALU.add))
            link(tt(passed[:, :, :], passed[:, :, :], cells(tiles_of[:, :].unsqueeze(1), by_tile), ALU.mult))
            link(nc.vector.tensor_reduce(tiles_before[:, :], passed[:, :, :], AX.X, ALU.add))
            tt(tile_in_region[:, :], tile_number[:, :], tiles_before[:, :], ALU.subtract)
            link(ts(tile_region[:, :], tile_expert[:, :], float(REGION), None, ALU.mult))
            stt(tile_row[:, :], tile_in_region[:, :], float(P), tile_region[:, :], ALU.mult, ALU.add)
            ts(tile_column[:, :], tile_expert[:, :], float(EXPERTS - 1), float(D), ALU.min, ALU.add)
            ts(tile_weights[:, :], tile_expert[:, :], float(EXPERTS - 1), float(HID), ALU.min,
               ALU.mult).then_inc(table_ready, 1)
            for c in (CHUNKS - 2, CHUNKS - 1):
                for piece in range(PIECES):
                    split(c, c, piece)

            def low_of_xs(t, n):
                dve.wait_ge(xsT_high, t + 1)
                tt(xsT[:, n % 2, 1, :], bank[6][:, 0:P], xsT[:, n % 2, 0, :].bitcast(F32),
                   ALU.subtract).then_inc(xsT_low, 1)

            def column_of(t):
                return dve.value_load(tile_column[0:1, bass.ds(t, 1)], min_val=D, max_val=D + EXPERTS - 1)

            def hidden_begin(t, n):
                dve.wait_ge(xs_in[n % RING], (t + 1 - (n % RING)) * (16 // RING) + (16 - 16 // RING))
                dve.wait_ge(y_free, t + 1)
                nc.vector.tensor_copy(add_to[:, n % RING:n % RING + 1], xs[:, n % RING, REC - 1:])

            def hidden(t, n, column):
                dve.wait_ge(up_done, t + 1)
                dve.wait_ge(gated_ready, t + 1)
                stt(hid[:, n % 2, :], gated[:, n % 2, :], xs[:, n % RING, bass.ds(column, 1)], bank[2 + n % 2][:, :],
                    ALU.mult, ALU.mult).then_inc(hid_ready, 1)

            def step(j, n, rest):
                if rest > 1:
                    column = column_of(j + 1)
                dve.wait_ge(high_transposed, j + 1)
                nc.vector.tensor_copy(hidT[:, HID // 2:], bank[5][:, 0:HID // 2]).then_inc(hidT_high, 1)
                if rest > 1:
                    hidden_begin(j + 1, n + 1)
                if rest > 2:
                    low_of_xs(j + 2, n + 2)
                if rest > 1:
                    hidden(j + 1, n + 1, column)
                dve.wait_ge(down_done, j + 1)
                nc.vector.tensor_copy(y[:, n, :], bank[7][:, 0:D]).then_inc(y_ready, 1)

            dve.wait_ge(table_ready, 1)
            low_of_xs(0, 0)
            low_of_xs(1, 1)
            hidden_begin(0, 0)
            hidden(0, 0, column_of(0))
            with dve.Fori(0, AHEAD // RING) as i:
                for n in range(RING):
                    step(i * RING + n, n, RING)
            for n in range(RING):
                step(AHEAD + n, n, RING - n)

            for c in range(LAST_CHUNKS):
                dve.wait_ge(sums_in[c], 32)
                first, second = (part[:, c] for part in sum_parts)
                tt(first, first, second, ALU.add).then_inc(out_ready, 1)

        @block.tensor
        def _(pe):
            mm = nc.tensor.matmul
            pe.wait_ge(shifts_ready, 1)

            def embed(taps, b):
                to = bank[b]
                whole = to[:, 0:SEQ].rearrange("p (t n) -> p t n", t=2)
                first, second = to[:, 0:D], to[:, D:SEQ]
                pair = taps[:, 2 * b:2 * b + 2, :]
                mm(whole, from_before[:, :], pair[:, :, 0:D], start=True, stop=False)
                mm(second, last_to_first[:, :], taps[:, 2 * b, 0:D], start=False, stop=False)
                mm(whole, ident[:, :], pair[:, :, D:2 * D], start=False, stop=False)
                mm(whole, from_after[:, :], pair[:, :, 2 * D:3 * D], start=False, stop=False)
                mm(first, first_to_last[:, :], taps[:, 2 * b + 1, 2 * D:3 * D],
                   start=False, stop=True).then_inc(embedded, 1)

            def to_scores(c, b, logits_before=None):
                pe.wait_ge(xn_ready, c * BC + b + 1)
                pe.wait_ge(xT_ready, c * BC + b)
                for t in range(2):
                    last = nc.tensor.transpose(bank[2][:, t * P:(t + 1) * P], xn[:, 2 * b + t, :], ident[:, :])
                last.then_inc(xn_transposed, 1)
                pe.wait_ge(xT_ready, c * BC + b + 1)
                pe.wait_ge(qT_ready, c * BC + b)
                if b == 0 and logits_before is not None:
                    pe.wait_ge(shifted_ready, logits_before)
                mm(bank[3][:, 0:SEQ], wqk_sb[:, :], xT[:, b % 2, :], start=True, stop=True).then_inc(q_done, 1)
                pe.wait_ge(v_ready, c * BC + b)
                for t in range(2):
                    last = mm(bank[5][:, t * D:(t + 1) * D], xT[:, b % 2, t * P:(t + 1) * P],
                              wvt_sb[:, :], start=True, stop=True)
                last.then_inc(v_done, 1)
                pe.wait_ge(qT_ready, c * BC + b + 1)
                pe.wait_ge(max_ready, c * BC + b)
                mm(bank[4][:, 0:P], qT[:, b % 2, 0:P], xT[:, b % 2, 0:P], start=True, stop=True)
                mm(bank[4][:, P:3 * P], qT[:, b % 2, P:], xT[:, b % 2, :],
                   start=True, stop=True).then_inc(scores_done, 1)

            def attend(c, b, places_before=None, taps=None):
                pe.wait_ge(probs_ready, c * BC + b + 1)
                pe.wait_ge(pT_ready, c * BC + b)
                if b == 0 and places_before is not None:
                    pe.wait_ge(rows_ready, places_before + 1)
                for n in range(3):
                    last = nc.tensor.transpose(bank[6][:, n * P:(n + 1) * P], probs[:, b % 2, n * P:(n + 1) * P],
                                               ident[:, :])
                last.then_inc(probs_transposed, 1)
                if taps is not None:
                    embed(taps, 0)
                pe.wait_ge(pT_ready, c * BC + b + 1)
                pe.wait_ge(v_ready, c * BC + b + 1)
                pe.wait_ge(h1_ready, c * BC + b)
                mm(bank[7][:, 0:D], pT[:, b % 2, 0:P], v[:, b % 2, 0:D], start=True, stop=True)
                mm(bank[7][:, D:SEQ], pT[:, b % 2, P:2 * P], v[:, b % 2, 0:D], start=True, stop=False)
                mm(bank[7][:, D:SEQ], pT[:, b % 2, 2 * P:], v[:, b % 2, D:],
                   start=False, stop=True).then_inc(pv_done, 1)

            def transpose_x2(k, embedded_before):
                pe.wait_ge(x2_ready, k + 1)
                pe.wait_ge(h_ready, embedded_before)
                for t in range(TC):
                    last = nc.tensor.transpose(bank[0][:, t * P:(t + 1) * P], x2[:, t, :], ident[:, :])
                last.then_inc(x2_transposed, 1)

            def route(k, queries_before):
                pe.wait_ge(qT_ready, queries_before)
                pe.wait_ge(x2T_ready, k + 1)
                wide = SETS * PER_GROUP
                for t in range(TC):
                    last = mm(bank[3][:, t * wide:(t + 1) * wide], x2T[:, t * P:(t + 1) * P], router_w[:, :],
                              start=True, stop=True)
                last.then_inc(logits_done, 1)

            def count_places(k, probs_before):
                pe.wait_ge(chosen_ready, k + 1)
                pe.wait_ge(pT_ready, probs_before)
                n = TC * EXPERTS
                mm(bank[6][:, 0:n], earlier[:, :], chosen[:, :, :].rearrange("p t e -> p (t e)"),
                   start=True, stop=False)
                for t in range(TC - 1):
                    mm(bank[6][:, (t + 1) * EXPERTS:n].rearrange("p (t e) -> p t e", e=EXPERTS), ones[:, :],
                       chosen[:, t:t + 1, :].broadcast_to([P, TC - 1 - t, EXPERTS]),
                       start=False, stop=(t == TC - 2))
                for t in range(TC):
                    last = mm(bank[6][:, n:n + EXPERTS], ones[:, :], chosen[:, t, :], start=(t == 0),
                              stop=(t == TC - 1))
                last.then_inc(places_done, 1)

            def prepare(k, a_too, routed, through):
                if a_too:
                    to_scores(k + 2, 0, k + 1)
                if routed:
                    count_places(k, k * BC + 2 * BC)
                transpose_x2(k + 1, through)
                if a_too:
                    to_scores(k + 2, 1)
                route(k + 1, through)

            per_chunk = 16 * TC
            for c in range(2):
                if c == 1:
                    pe.wait_ge(h_ready, BC)
                pe.wait_ge(gathered[c], per_chunk)
                for b in range(BC):
                    embed(taps_at[c], b)
            pe.wait_ge(front_weights_in, 16 * 7)
            pe.wait_ge(constants_ready, 1)
            for b in range(BC):
                to_scores(0, b)
            for b in range(BC):
                attend(0, b)

            def step(k, taps, landed, rows, routed):
                pe.wait_ge(landed, rows)
                pe.wait_ge(h_ready, k * BC + 2 * BC)
                embed(taps, 1)
                prepare(k - 1, True, routed, k * BC + 2 * BC)
                attend(k + 1, 0, k, taps)
                attend(k + 1, 1)

            for k in range(2):
                step(k, taps_at[k + 2], gathered[k + 2], per_chunk, k > 0)
            with pe.Fori(0, FRONT - 1) as i:
                for par in range(2):
                    step(i * 2 + (2 + par), taps_of[:, par], gathered[4 + par], i * per_chunk + per_chunk, True)
            prepare(CHUNKS - 3, True, True, CHUNKS * BC)
            attend(CHUNKS - 1, 0, CHUNKS - 2)
            attend(CHUNKS - 1, 1)
            prepare(CHUNKS - 2, False, True, CHUNKS * BC)
            count_places(CHUNKS - 1, CHUNKS * BC)

            pe.wait_ge(table_ready, 1)
            pe.wait_ge(low_ready, CHUNKS * PIECES)
            pe.wait_ge(w2_in, 16 * CHUNKS)

            most = (EXPERTS - 1) * HID
            carried = [pe.alloc_register(f"weights_at{n}") for n in range(2)]

            def weights_at(t):
                return pe.value_load(tile_weights[0:1, bass.ds(t, 1)], min_val=0, max_val=most)

            def carry(t, n):
                pe.reg_load(carried[n], tile_weights[0:1, bass.ds(t, 1)])

            def transpose_xs(t, n):
                pe.wait_ge(xs_in[n % RING], (t + 1 - (n % RING)) * (16 // RING) + (16 - 16 // RING))
                nc.tensor.transpose(bank[6][:, 0:P], xs[:, n % RING, 0:D],
                                    ident[:, :]).then_inc(xs_transposed, 1)

            def product(to, n, which, at):
                high, low = w_high[which][:, bass.ds(at, HID)], w_low[which][:, bass.ds(at, HID)]
                mm(to, xsT[:, n % 2, 0, :], high, start=True, stop=False)
                mm(to, xsT[:, n % 2, 0, :], low, start=False, stop=False)
                return mm(to, xsT[:, n % 2, 1, :], high, start=False, stop=True)

            def gate(t, n, at):
                pe.wait_ge(xsT_low, t + 1)
                product(bank[n % 2][:, :], n, 0, at).then_inc(gate_done, 1)

            def up(n, at):
                product(bank[2 + n % 2][:, :], n, 1, at).then_inc(up_done, 1)

            def step(j, n, at, rest):
                if rest > 1:
                    gate(j + 1, n + 1, at[n + 1])
                pe.wait_ge(hid_ready, j + 1)
                for half, transposed in ((0, low_transposed), (1, high_transposed)):
                    for k in range(HK // 2):
                        at_k = (half * HK // 2 + k) * P
                        last = nc.tensor.transpose(bank[4 + half][:, k * P:(k + 1) * P],
                                                   hid[:, n % 2, at_k:at_k + P], ident[:, :])
                    last.then_inc(transposed, 1)
                if rest > 2:
                    transpose_xs(j + 2, n + 2)
                if rest > 1:
                    up(n + 1, at[n + 1])
                if rest > 2:
                    if n + 2 <= RING:
                        at.append(weights_at(j + 2))
                    if n + 2 >= RING:
                        carry(j + 2, n + 2 - RING)
                for k in range(HK):
                    if k == 0:
                        pe.wait_ge(hidT_low, j + 1)
                        pe.wait_ge(y_ready, j + 1)
                    elif k == HK // 2:
                        pe.wait_ge(hidT_high, j + 1)
                    last = mm(bank[7][:, 0:D], hidT[:, k * P:(k + 1) * P],
                              w2_sb[:, bass.ds(at[n] + k * D, D)], start=(k == 0), stop=(k == HK - 1))
                last.then_inc(down_done, 1)

            carry(0, 0)
            carry(1, 1)
            first_at = weights_at(0)
            transpose_xs(0, 0)
            pe.wait_ge(xsT_low, 1)
            transpose_xs(1, 1)
            gate(0, 0, first_at)
            up(0, first_at)

            def taken():
                return [pe.snap(r, min_val=0, max_val=most) for r in carried]

            with pe.Fori(0, AHEAD // RING) as i:
                at = taken()
                for n in range(RING):
                    step(i * RING + n, n, at, RING)
            at = taken()
            for n in range(RING):
                step(AHEAD + n, n, at, RING - n)


def kernel(x, L0_tok_conv_w, L0_attn_W_qk, L0_attn_W_v, L0_attn_b_v, L0_ffn_Wr, L0_ffn_br, L0_ffn_Wgate,
           L0_ffn_bgate, L0_ffn_W1, L0_ffn_W3, L0_ffn_W2):
    import numpy as np
    import concourse.bacc as bacc
    from concourse.bass_utils import run_bass_kernel_spmd

    lay = np.ascontiguousarray
    arrays = {
        "ids": lay(np.asarray(x).reshape(TILES_IN, P).T),
        "embedding": lay(np.asarray(L0_tok_conv_w).transpose(1, 2, 0).reshape(VOCAB, TAPS * D)),
        "w_qk": lay(L0_attn_W_qk),
        "w_v_t": lay(np.asarray(L0_attn_W_v).T),
        "b_v": lay(L0_attn_b_v),
        "w_route": lay(L0_ffn_Wr),
        "w_gate": lay(np.asarray(L0_ffn_Wgate).transpose(1, 0, 2).reshape(D, EXPERTS)),
        "b_route": lay(L0_ffn_br),
        "b_gate": lay(np.asarray(L0_ffn_bgate).reshape(EXPERTS)),
        "w1": lay(np.asarray(L0_ffn_W1).transpose(1, 0, 2).reshape(D, EXPERTS * HID)),
        "w3": lay(np.asarray(L0_ffn_W3).transpose(1, 0, 2).reshape(D, EXPERTS * HID)),
        "w2": lay(np.asarray(L0_ffn_W2).reshape(EXPERTS, HK, P, D).transpose(2, 0, 1, 3).reshape(P, -1)),
    }
    nc = bacc.Bacc("TRN2", target_bir_lowering=False, num_devices=1)
    args = [nc.dram_tensor(name, a.shape, mybir.dt.from_np(a.dtype), kind="ExternalInput").ap()
            for name, a in arrays.items()]
    out = nc.dram_tensor("out", [BATCHES, SEQ, D], F32, kind="ExternalOutput").ap()
    tower_kernel(nc, *args, out)
    return run_bass_kernel_spmd(nc, [arrays], core_ids=[0]).results[0]["out"]
```
